# Optimizing a Trainium2 kernel written in Bass

```python
import numpy as np
import jax
import jax.numpy as jnp

def _softmax(x, axis=-1):
    return jax.nn.softmax(x, axis=axis)

def _gelu(x):
    return jax.nn.gelu(x, approximate=True)

def _silu(x):
    return jax.nn.silu(x)

def _sigmoid(x):
    return jax.nn.sigmoid(x)

def _layernorm(x, axis=-1, eps=1e-05):
    m = jnp.mean(x, axis=axis, keepdims=True)
    v = jnp.var(x, axis=axis, keepdims=True)
    return (x - m) / jnp.sqrt(v + eps)

def _scatter_add(tgt, idx, src, axis=0):
    return tgt.at[idx].add(src)

def _segment_sum(src, seg, n):
    return jax.ops.segment_sum(src, seg, n)
kernel_name = 'mk_adj_preln_d2_adj_r2_6bee4f'

def setup_inputs(seed: int=0):
    np.random.seed(seed)
    _w = jnp.asarray

    def _rec_inputs():
        import jax
        import jax.numpy as jnp
        _gk = jax.random.key(seed)
        x = -1.394e-06 + 0.9999 * jax.random.normal(jax.random.fold_in(_gk, 1), (16, 512, 256), jnp.float32)
        _a = jax.random.bernoulli(jax.random.fold_in(_gk, 2), 0.0078125, (16, 512, 512))
        _a = jnp.logical_or(_a, jnp.swapaxes(_a, -1, -2))
        _a = jnp.logical_or(_a, jnp.eye(512, dtype=bool))
        adj = _a.astype(jnp.int32)
        return (x, adj)
    x, adj = _rec_inputs()

    def _L0_gnn_setup():
        import jax, jax.numpy as jnp
        import numpy as np
        NEG_INF = -1000000000.0
        NEG_SLOPE = 0.2

        def gat_layer(x, mask, W, a_src, a_dst, bias, concat):
            B, N, _ = x.shape
            H, F = a_src.shape
            xl = (x @ W).reshape(B, N, H, F)
            asrc = jnp.einsum('bnhf,hf->bnh', xl, a_src)
            adst = jnp.einsum('bnhf,hf->bnh', xl, a_dst)
            e = jax.nn.leaky_relu(asrc[:, :, None, :] + adst[:, None, :, :], NEG_SLOPE)
            e = jnp.where(mask[..., None], e, NEG_INF)
            attn = jax.nn.softmax(e, axis=1)
            out = jnp.einsum('bsdh,bshf->bdhf', attn, xl)
            if concat:
                out = out.reshape(B, N, H * F)
            else:
                out = out.mean(axis=2)
            return out + bias
        key = jax.random.key(seed)
        ks = jax.random.split(key, 10)
        B, N, Din, Fh, H, Dout = (8, 512, 256, 128, 4, 256)
        s = 0.05
        return {'adj': jax.random.randint(ks[0], (B, N, N), 0, 2, dtype=jnp.int32), 'x': jax.random.normal(ks[1], (B, N, Din), dtype=jnp.float32), 'W1': jax.random.normal(ks[2], (Din, H * Fh), dtype=jnp.float32) * s, 'att_src1': jax.random.normal(ks[3], (H, Fh), dtype=jnp.float32) * s, 'att_dst1': jax.random.normal(ks[4], (H, Fh), dtype=jnp.float32) * s, 'b1': jax.random.normal(ks[5], (H * Fh,), dtype=jnp.float32) * s, 'W2': jax.random.normal(ks[6], (H * Fh, Dout), dtype=jnp.float32) * s, 'att_src2': jax.random.normal(ks[7], (1, Dout), dtype=jnp.float32) * s, 'att_dst2': jax.random.normal(ks[8], (1, Dout), dtype=jnp.float32) * s, 'b2': jax.random.normal(ks[9], (Dout,), dtype=jnp.float32) * s}
    _L0_gnn_all = _L0_gnn_setup()
    _L0_gnn_in = {k: v for k, v in _L0_gnn_all.items() if k in ('W1', 'att_src1', 'att_dst1', 'b1', 'W2', 'att_src2', 'att_dst2', 'b2')}
    del _L0_gnn_all

    def _L1_gnn_setup():
        import jax, jax.numpy as jnp
        import numpy as np
        ALPHA = 0.2

        def _leaky(x):
            return jnp.where(x >= 0, x, ALPHA * x)
        key = jax.random.key(seed)
        k1, k2, k3, k4 = jax.random.split(key, 4)
        B, N, F_in, F_out = (4, 1024, 256, 256)
        h = jax.random.normal(k1, (B, N, F_in), dtype=jnp.float32)
        W = jax.random.normal(k2, (F_in, F_out), dtype=jnp.float32) * 0.05
        a = jax.random.normal(k3, (2 * F_out, 1), dtype=jnp.float32) * 0.05
        adj = jax.random.randint(k4, (B, N, N), 0, 2, dtype=jnp.int32)
        return {'h': h, 'W': W, 'a': a, 'adj': adj}
    _L1_gnn_all = _L1_gnn_setup()
    _L1_gnn_in = {k: v for k, v in _L1_gnn_all.items() if k in ('W', 'a')}
    del _L1_gnn_all
    return {'x': x, 'adj': adj, 'L0_gnn_W1': _L0_gnn_in['W1'], 'L0_gnn_att_src1': _L0_gnn_in['att_src1'], 'L0_gnn_att_dst1': _L0_gnn_in['att_dst1'], 'L0_gnn_b1': _L0_gnn_in['b1'], 'L0_gnn_W2': _L0_gnn_in['W2'], 'L0_gnn_att_src2': _L0_gnn_in['att_src2'], 'L0_gnn_att_dst2': _L0_gnn_in['att_dst2'], 'L0_gnn_b2': _L0_gnn_in['b2'], 'L1_gnn_W': _L1_gnn_in['W'], 'L1_gnn_a': _L1_gnn_in['a']}

def reference(x, adj, L0_gnn_W1, L0_gnn_att_src1, L0_gnn_att_dst1, L0_gnn_b1, L0_gnn_W2, L0_gnn_att_src2, L0_gnn_att_dst2, L0_gnn_b2, L1_gnn_W, L1_gnn_a):
    import jax
    import jax.numpy as jnp

    def _L0_gnn_ref(adj, x, W1, att_src1, att_dst1, b1, W2, att_src2, att_dst2, b2):
        import jax, jax.numpy as jnp
        import numpy as np
        NEG_INF = -1000000000.0
        NEG_SLOPE = 0.2

        def gat_layer(x, mask, W, a_src, a_dst, bias, concat):
            B, N, _ = x.shape
            H, F = a_src.shape
            xl = (x @ W).reshape(B, N, H, F)
            asrc = jnp.einsum('bnhf,hf->bnh', xl, a_src)
            adst = jnp.einsum('bnhf,hf->bnh', xl, a_dst)
            e = jax.nn.leaky_relu(asrc[:, :, None, :] + adst[:, None, :, :], NEG_SLOPE)
            e = jnp.where(mask[..., None], e, NEG_INF)
            attn = jax.nn.softmax(e, axis=1)
            out = jnp.einsum('bsdh,bshf->bdhf', attn, xl)
            if concat:
                out = out.reshape(B, N, H * F)
            else:
                out = out.mean(axis=2)
            return out + bias
        B, N, _ = adj.shape
        mask = (adj > 0) | jnp.eye(N, dtype=bool)[None]
        h = jax.nn.elu(gat_layer(x, mask, W1, att_src1, att_dst1, b1, concat=True))
        h = gat_layer(h, mask, W2, att_src2, att_dst2, b2, concat=False)
        return h

    def _L1_gnn_ref(h, W, a, adj):
        import jax, jax.numpy as jnp
        import numpy as np
        ALPHA = 0.2

        def _leaky(x):
            return jnp.where(x >= 0, x, ALPHA * x)
        F_out = W.shape[1]
        Wh = jnp.matmul(h, W)
        Wh_sg = jax.lax.stop_gradient(Wh)
        a1 = a[:F_out, 0]
        a2 = a[F_out:, 0]
        s_i = Wh_sg @ a1
        s_j = Wh_sg @ a2
        e = _leaky(s_i[:, :, None] + s_j[:, None, :])
        e = jnp.where(adj > 0, e, jnp.float32(-9000000000000000.0))
        attention = jax.nn.softmax(e, axis=1)
        h_prime = jnp.einsum('bij,bjf->bif', attention, Wh)
        return _leaky(h_prime)
    h = jnp.maximum(_layernorm(x, axis=-1), 0.0)
    x = x + _L0_gnn_ref(adj, h, L0_gnn_W1, L0_gnn_att_src1, L0_gnn_att_dst1, L0_gnn_b1, L0_gnn_W2, L0_gnn_att_src2, L0_gnn_att_dst2, L0_gnn_b2)
    h = jnp.maximum(_layernorm(x, axis=-1), 0.0)
    x = x + _L1_gnn_ref(h, L1_gnn_W, L1_gnn_a, adj)
    return x

_drawn_inputs = setup_inputs


def setup_inputs(seed=0):
    import zlib

    import numpy as np

    out = dict(_drawn_inputs(seed))
    spreads = {}
    factors = {'L0_gnn_att_src1': 4.207,
     'L0_gnn_att_dst1': 8.0,
     'L0_gnn_att_src2': 8.0,
     'L0_gnn_att_dst2': 28.46}
    for name, (base, spread) in spreads.items():
        noise = np.random.default_rng([zlib.crc32(name.encode()), seed]).standard_normal(out[name].shape)
        drawn = base * np.exp(spread * noise) if base else spread * noise
        out[name] = jnp.asarray(drawn.astype(out[name].dtype))
    for name, factor in factors.items():
        out[name] = (out[name] * factor).astype(out[name].dtype)
    return out
```

```python
from contextlib import ExitStack
from typing import NamedTuple

import concourse.bass as bass
from concourse import mybir

P = 128
F32 = mybir.dt.float32
F32R = mybir.dt.float32r
BF16 = mybir.dt.bfloat16
I32 = mybir.dt.int32
ALU = mybir.AluOpType
ACT = mybir.ActivationFunctionType
AX = mybir.AxisListType

BATCHES = 16
NODES = 512
DIM = 256
HEADS = 4
HEAD_DIM = 128
WIDE = HEADS * HEAD_DIM
NC = NODES // P
KC = DIM // P
EPS = 1e-5
SETTLED_FRONT = 12
SETTLED_BACK = 12
SLOPE = 0.2
FALL = 1.0 - SLOPE


class Batch(NamedTuple):
    n: object
    half: object
    slot: int

    def after(self, m):
        return not isinstance(self.n, int) or self.n >= m


class Ring:

    def __init__(self, *order):
        self.order = order
        self.front = sum(c for _, part, c in order if part == "front")
        self.whole = sum(c for _, _, c in order)
        assert self.front % 2 == 0 and self.whole % 2 == 0

    def use(self, back, front, name, i):
        at = 0
        for what, part, count in self.order:
            if what == name:
                break
            if (back if part == "back" else front) is not None:
                at += count
        base = 0 if back is None else back.n * self.whole + self.front
        return base + at + i, (at + i) % 2


def older(use):
    return not isinstance(use, int) or use >= 2


TURN = Ring(("hn1", "front", KC), ("mask", "front", 2), ("hn2", "back", KC), ("elu", "front", HEADS))
PROJ = Ring(("proj2", "back", NC), ("proj1", "front", 2 * NC), ("proj3", "back", NC))
SUMS = Ring(("sum2", "back", NC), ("sum1", "front", 2 * HEADS), ("sum3", "back", 2))
ROWS = Ring(("rows2", "back", 1), ("shift2", "back", 1), ("q2", "back", 1),
            ("rows1", "front", 1), ("shift1", "front", 1), ("q1", "front", HEADS),
            ("rows3", "back", 1), ("shift3", "back", 1), ("q3", "back", 1))
PROB = Ring(("p2", "back", 1), ("p1", "front", HEADS), ("p3", "back", 1))


def steps(engine, step):
    step(None, Batch(0, 0, 0))
    step(Batch(0, 0, 0), Batch(1, 0, 1))
    with engine.Fori(0, (BATCHES - 2) // 2) as i:
        step(Batch(i * 2 + 1, i, 1), Batch(i * 2 + 2, i + 1, 0))
        step(Batch(i * 2 + 2, i + 1, 0), Batch(i * 2 + 3, i + 1, 1))
    step(Batch(BATCHES - 1, BATCHES // 2 - 1, 1), None)


def gat_block(nc, x, adj, W1, src1, dst1, b1, W2, src2, dst2, b2, W3, a3, out):
    with ExitStack() as ctx:
        def sb(name, shape, dt=F32):
            return ctx.enter_context(nc.sbuf_tensor(name, shape, dt))

        def bank(name):
            return ctx.enter_context(nc.psum_tensor(name, [P, 512], F32))

        def sem(name):
            return ctx.enter_context(nc.semaphore(name))

        ident = sb("ident", [P, P])
        ident_b = sb("ident_b", [P, P], BF16)
        ones = sb("ones", [P, P])
        pick_f = sb("pick_f", [P, HEADS, P])
        pick = sb("pick", [P, HEADS, P], F32R)
        w1 = sb("w1", [P, KC, 2, 260])
        w2 = sb("w2", [P, NC, DIM + 2])
        w3 = sb("w3", [P, KC, DIM + 2])
        att1 = sb("att1", [P, 2, WIDE])
        att2 = sb("att2", [P, 2, DIM])
        att3 = sb("att3", [P, 2, DIM])
        bias1 = sb("bias1", [P, WIDE])
        bias2 = sb("bias2", [P, DIM])
        minus_one = sb("minus_one", [P, 1])
        eps = sb("eps", [P, NC])
        half_power = sb("half_power", [P, NC])

        x_in = [sb(f"x_in{s}", [P, NC, DIM]) for s in range(2)]
        adj_in = [sb(f"adj_in{s}", [P, NC, NODES], I32) for s in range(2)]
        xb = [sb(f"xb{s}", [P, NC, DIM]) for s in range(2)]
        mask = [sb(f"mask{s}", [P, NC, NODES], BF16) for s in range(2)]
        maskT = [sb(f"maskT{s}", [P, NC, NODES], BF16) for s in range(2)]
        count = [sb(f"count{s}", [P, NC]) for s in range(2)]
        keep = sb("keep", [P, NC])
        empty = sb("empty", [P, NC])

        class Norm:
            def __init__(self, name):
                self.halves = sb(f"halves_{name}", [P, NC, 6])
                self.stats = sb(f"stats_{name}", [P, NC, 2])
                self.var = sb(f"var_{name}", [P, NC])
                self.rstd = sb(f"rstd_{name}", [P, NC])
                self.out = sb(f"hn_{name}", [P, NC, DIM])
                self.T = sb(f"hT_{name}", [P, KC, NODES])

        norm1, norm2 = Norm("1"), Norm("2")

        class Scores:
            def __init__(self, name, heads):
                self.heads = heads
                self.cols = sb(f"cols_{name}", [P, NC, P])
                self.neg = sb(f"neg_{name}", [P, 1])
                self.diag = sb(f"diag_{name}", [P, HEADS])
                self.row = sb(f"row_{name}", [P, NODES])
                self.q = sb(f"q_{name}", [P, NODES])
                self.split = sb(f"split_{name}", [P, NODES], F32R)
                self.rel = sb(f"rel_{name}", [P, NC, heads])
                self.r = sb(f"r_{name}", [P, NC, heads])

        sc1, sc2, sc3 = Scores("1", HEADS), Scores("2", 1), Scores("3", 1)
        xl1 = sb("xl1", [P, NC, 2, 260])
        y1 = sb("y1", [P, NC, HEADS, HEAD_DIM + 1])
        xl2 = sb("xl2", [P, NC, DIM + 2])
        y2 = sb("y2", [P, NC, DIM + 1])
        xl3 = sb("xl3", [P, NC, DIM + 2])
        y3 = sb("y3", [P, NC, DIM])
        prob = [sb(f"prob{s}", [P, NC, NODES]) for s in range(2)]
        rz1 = sb("rz1", [P, 2 * HEADS, 2])
        z1 = [sb(f"z1_{s}", [P, NC, HEAD_DIM]) for s in range(2)]
        ez = [sb(f"ez_{s}", [P, NC, HEAD_DIM]) for s in range(2)]
        elu = [sb(f"elu_{s}", [P, NC, HEAD_DIM]) for s in range(2)]
        h2T = sb("h2T", [P, HEADS, NODES])
        rz2 = sb("rz2", [P, NC])
        x1 = sb("x1", [P, NC, DIM])
        low_row = sb("low_row", [P, NODES])
        low_col = sb("low_col", [P, NC])
        expo = sb("expo", [P, NC, NODES])
        z3 = sb("z3", [P, NC])
        rz3 = sb("rz3", [P, NC])
        small = sb("small", [P, NC, DIM])
        o = sb("o", [P, NC, DIM])

        turn_b = [bank(f"turn{i}") for i in range(2)]
        proj_b = [bank(f"proj{i}") for i in range(2)]
        sums_b = [bank(f"sums{i}") for i in range(2)]
        rows_b = [bank(f"rows{i}") for i in range(2)]

        w_loaded = sem("w_loaded")
        x_loaded = [sem(f"x_loaded{s}") for s in range(2)]
        adj_loaded = [sem(f"adj_loaded{s}") for s in range(2)]
        out_stored = sem("out_stored")
        pool_consts = sem("pool_consts")
        dve_ready = sem("dve_ready")
        dve_settled = sem("dve_settled")
        pool_settled = sem("pool_settled")
        mask_made = sem("mask_made")
        xb_made = sem("xb_made")
        var_made = [sem(f"var_made{i}") for i in range(2)]
        rstd_made = [sem(f"rstd_made{i}") for i in range(2)]
        hn_made = [sem(f"hn_made{i}") for i in range(2)]
        turn_full, turn_free = sem("turn_full"), sem("turn_free")
        proj_full, proj_free = sem("proj_full"), sem("proj_free")
        sums_full, sums_free = sem("sums_full"), sem("sums_free")
        rows_full, rows_free = sem("rows_full"), sem("rows_free")
        prob_full = sem("prob_full")
        cols_made = [sem(f"cols_made{i}") for i in range(3)]
        diag_made = [sem(f"diag_made{i}") for i in range(3)]
        q_made = [sem(f"q_made{i}") for i in range(2)]
        split_made = [sem(f"split_made{i}") for i in range(3)]
        r_made = [sem(f"r_made{i}") for i in range(2)]
        y1_made = sem("y1_made")
        y2_made = sem("y2_made")
        y3_made = sem("y3_made")
        ez_made = sem("ez_made")
        elu_made = sem("elu_made")
        low_row_made = sem("low_row_made")
        expo_made = sem("expo_made")
        e3_made = sem("e3_made")
        rz3_made = sem("rz3_made")
        small_made = sem("small_made")
        out_made = sem("out_made")

        x_v = x.rearrange("b (c p) d -> b p c d", p=P)
        adj_v = adj.rearrange("b (c p) d -> b p c d", p=P)
        out_v = out.rearrange("b (c p) d -> b p c d", p=P)

        def spread(row):
            return row.to_broadcast([P, row.shape[1]])

        block = ctx.enter_context(nc.Block())

        @block.sync
        def _(sp):
            sp.dma_start(x_in[0][:], x_v[0]).then_inc(x_loaded[0], 16)
            sp.dma_start(adj_in[0][:], adj_v[0]).then_inc(adj_loaded[0], 16)
            for g in range(2):
                sp.dma_start(w1[:, :, g, 0:256], W1.rearrange("(c p) n -> p c n", p=P)[:, :, g * 256:g * 256 + 256]
                             ).then_inc(w_loaded, 16)
            sp.dma_start(att1[:, 0, :], spread(src1.rearrange("(o h) f -> o (h f)", o=1))).then_inc(w_loaded, 16)
            sp.dma_start(att1[:, 1, :], spread(dst1.rearrange("(o h) f -> o (h f)", o=1))).then_inc(w_loaded, 16)
            sp.dma_start(w2[:, :, 0:DIM], W2.rearrange("(c p) n -> p c n", p=P)).then_inc(w_loaded, 16)
            sp.dma_start(att2[:, 0, :], spread(src2)).then_inc(w_loaded, 16)
            sp.dma_start(att2[:, 1, :], spread(dst2)).then_inc(w_loaded, 16)
            sp.dma_start(w3[:, :, 0:DIM], W3.rearrange("(c p) n -> p c n", p=P)).then_inc(w_loaded, 16)
            a3_v = a3.rearrange("(t f) o -> t (f o)", t=2)
            sp.dma_start(att3[:, 0, :], spread(a3_v[0:1, :])).then_inc(w_loaded, 16)
            sp.dma_start(att3[:, 1, :], spread(a3_v[1:2, :])).then_inc(w_loaded, 16)
            sp.dma_start(bias1[:], spread(b1.rearrange("(o n) -> o n", o=1))).then_inc(w_loaded, 16)
            sp.dma_start(bias2[:], spread(b2.rearrange("(o n) -> o n", o=1))).then_inc(w_loaded, 16)
            sp.dma_start(x_in[1][:], x_v[1]).then_inc(x_loaded[1], 16)
            sp.dma_start(adj_in[1][:], adj_v[1]).then_inc(adj_loaded[1], 16)

            def store(b):
                sp.wait_ge(out_made, b.n + 1)
                sp.dma_start(out_v[b.n], o[:]).then_inc(out_stored, 16)

            with sp.Fori(0, (BATCHES - 2) // 2) as i:
                for s in range(2):
                    b = Batch(i * 2 + s, i, s)
                    sp.wait_ge(hn_made[0], b.n + 1)
                    sp.wait_ge(xb_made, b.n + 1)
                    sp.dma_start(x_in[s][:], x_v[b.n + 2]).then_inc(x_loaded[s], 16)
                    sp.wait_ge(mask_made, b.n + 1)
                    sp.dma_start(adj_in[s][:], adj_v[b.n + 2]).then_inc(adj_loaded[s], 16)
                    store(b)
            store(Batch(BATCHES - 2, 0, 0))
            store(Batch(BATCHES - 1, 0, 1))
            sp.wait_ge(out_stored, 16 * BATCHES)

        @block.gpsimd
        def _(pool):
            nc.gpsimd.memset(ident[:], 0.0).then_inc(pool_settled, 1)
            nc.gpsimd.memset(pick_f[:], 0.0).then_inc(pool_settled, 1)
            nc.gpsimd.memset(half_power[:], -0.5)
            nc.gpsimd.memset(eps[:], EPS)
            pool.wait_ge(pool_settled, 2)
            nc.gpsimd.affine_select(out=ident[:], in_=ident[:], compare_op=ALU.not_equal, fill=1.0, base=0,
                                    pattern=[[-1, P]], channel_multiplier=1).then_inc(pool_consts, 1)
            for lift in (0, 32):
                nc.gpsimd.affine_select(out=pick_f[:], in_=pick_f[:], compare_op=ALU.not_equal, fill=1.0, base=-lift,
                                        pattern=[[-1, HEADS], [0, P]], channel_multiplier=1).then_inc(pool_settled, 1)
                pool.wait_ge(pool_settled, 3 + lift // 32)
            nc.gpsimd.tensor_copy(pick[:], pick_f[:]).then_inc(pool_consts, 1)
            settled = [4]

            def rstd(b, which, norm):
                pool.wait_ge(var_made[which], b.n + 1)
                nc.gpsimd.tensor_tensor(norm.var[:], norm.stats[:, :, 1], eps[:], ALU.add
                                        ).then_inc(pool_settled, 1)
                settled[0] = settled[0] + 1
                pool.wait_ge(pool_settled, settled[0])
                nc.gpsimd.tensor_tensor(norm.rstd[:], norm.var[:], half_power[:], ALU.pow
                                        ).then_inc(rstd_made[which], 1)

            def step(back, front):
                if back is not None:
                    settled[0] = back.n * 2 + 5
                if front is not None:
                    rstd(front, 0, norm1)
                    if back is None:
                        pool.wait_ge(w_loaded, 16 * 12)
                    pool.wait_ge(x_loaded[front.slot], front.half * 16 + 16)
                    nc.gpsimd.tensor_tensor(xb[front.slot][:], x_in[front.slot][:],
                                            bias2[:, None, :].to_broadcast([P, NC, DIM]), ALU.add
                                            ).then_inc(xb_made, 1)
                    pool.wait_ge(r_made[0], front.n + 1)
                    for h in range(HEADS):
                        g, at = h // 2, h % 2 * HEAD_DIM
                        nc.gpsimd.tensor_tensor(
                            y1[:, :, h, 0:HEAD_DIM], xl1[:, :, g, at:at + HEAD_DIM],
                            y1[:, :, h, HEAD_DIM:HEAD_DIM + 1].to_broadcast([P, NC, HEAD_DIM]), ALU.mult
                        ).then_inc(y1_made, 1)
                if back is not None:
                    rstd(back, 1, norm2)
                    use, _ = SUMS.use(back, front, "sum3", 1)
                    pool.wait_ge(sums_free, use + 1)
                    if back.after(1):
                        pool.wait_ge(out_stored, back.n * 16)
                    nc.gpsimd.tensor_tensor(o[:], small[:], x1[:], ALU.add).then_inc(out_made, 1)

            steps(pool, step)

        @block.scalar
        def _(act):
            def from_proj(back, front, name, i, dst):
                use, b = PROJ.use(back, front, name, i)
                act.wait_ge(proj_full, use + 1)
                n = dst.shape[-1]
                nc.scalar.copy(dst, proj_b[b][:, 0:n]).then_inc(proj_free, 1)

            def relu_turned(back, front, name, norm):
                for c in range(KC):
                    use, b = TURN.use(back, front, name, c)
                    act.wait_ge(turn_full, use + 1)
                    nc.scalar.activation(norm.T[:, c, :], turn_b[b][:], ACT.Relu).then_inc(turn_free, 1)

            def q_row(back, front, name, which, sc):
                use, _ = ROWS.use(back, front, "rows" + name, 0)
                act.wait_ge(rows_free, use + 1)
                nc.scalar.activation(sc.q[32:32 + sc.heads, :], sc.row[32:32 + sc.heads, :], ACT.Exp, scale=-FALL
                                     ).then_inc(q_made[which], 1)

            def r_cols(back, front, name, which, sc, low):
                use, _ = ROWS.use(back, front, "shift" + name, 0)
                act.wait_ge(rows_free, use + 1)
                nc.scalar.activation(sc.r[:], sc.rel[:], ACT.Exp, scale=FALL)
                nc.scalar.activation(low, sc.rel[:], ACT.Exp, scale=SLOPE).then_inc(r_made[which], 1)

            def elu_exp(back, front, h):
                use, _ = SUMS.use(back, front, "sum1", 2 * h + 1)
                act.wait_ge(sums_free, use + 1)
                nc.scalar.activation(ez[h % 2][:], z1[h % 2][:], ACT.Exp, bias=minus_one[:]).then_inc(ez_made, 1)

            def elu_turned(back, front, h):
                use, b = TURN.use(back, front, "elu", h)
                act.wait_ge(turn_full, use + 1)
                nc.scalar.activation(h2T[:, h, :], turn_b[b][:], ACT.Identity, bias=minus_one[:]
                                     ).then_inc(turn_free, 1)

            def step(back, front):
                if back is not None:
                    for c in range(NC):
                        from_proj(back, front, "proj2", c, xl2[:, c, :])
                if front is not None:
                    relu_turned(back, front, "hn1", norm1)
                    for c in range(NC):
                        use, b = TURN.use(back, front, "mask", c // 2)
                        if c % 2 == 0:
                            act.wait_ge(turn_full, use + 1)
                        at = c % 2 * NODES
                        last = nc.scalar.activation(maskT[front.slot][:, c, :],
                                                    turn_b[b][:].bitcast(BF16)[:, at:at + NODES], ACT.Copy,
                                                    accum_out=count[front.slot][:, c:c + 1])
                        if c % 2:
                            last.then_inc(turn_free, 1)
                    if front.after(1):
                        act.wait_ge(y1_made, front.n * HEADS)
                    for i in range(2):
                        from_proj(back, front, "proj1", i, xl1[:, i // 2, i % 2, :])
                if back is not None:
                    q_row(back, front, "2", 1, sc2)
                if front is not None:
                    for i in range(2, 4):
                        from_proj(back, front, "proj1", i, xl1[:, i // 2, i % 2, :])
                if back is not None:
                    r_cols(back, front, "2", 1, sc2, y2[:, :, DIM:DIM + 1])
                    act.wait_ge(r_made[1], back.n + 1)
                    for c in range(NC):
                        nc.scalar.activation(y2[:, c, 0:DIM], xl2[:, c, 0:DIM], ACT.Copy,
                                             scale=y2[:, c, DIM:DIM + 1]).then_inc(y2_made, 1)
                if front is not None:
                    for i in range(4, 8):
                        from_proj(back, front, "proj1", i, xl1[:, i // 2, i % 2, :])
                    q_row(back, front, "1", 0, sc1)
                    r_cols(back, front, "1", 0, sc1, y1[:, :, :, HEAD_DIM])
                    elu_exp(back, front, 0)
                if back is not None:
                    relu_turned(back, front, "hn2", norm2)
                if front is not None:
                    elu_turned(back, front, 0)
                if back is not None:
                    for c in range(NC):
                        from_proj(back, front, "proj3", c, xl3[:, c, :])
                if front is not None:
                    elu_exp(back, front, 1)
                    elu_turned(back, front, 1)
                    elu_exp(back, front, 2)
                if back is not None:
                    use, b = ROWS.use(back, front, "q3", 0)
                    act.wait_ge(rows_full, use + 1)
                    nc.scalar.activation(low_row[:], rows_b[b][:], ACT.Copy, scale=SLOPE).then_inc(low_row_made, 1)
                    for c in range(NC):
                        act.wait_ge(expo_made, back.n * NC + (c + 1))
                        nc.scalar.activation(expo[:, c, :], expo[:, c, :], ACT.Exp, scale=keep[:, c:c + 1]
                                             ).then_inc(e3_made, 1)
                    for c in range(NC):
                        act.wait_ge(rz3_made, back.n * NC + (c + 1))
                        nc.scalar.activation(y3[:, c, :], xl3[:, c, 0:DIM], ACT.Copy, scale=rz3[:, c:c + 1]
                                             ).then_inc(y3_made, 1)
                if front is not None:
                    elu_turned(back, front, 2)
                    elu_exp(back, front, 3)
                for a in range(2):
                    if back is not None:
                        use, b = SUMS.use(back, front, "sum3", a)
                        act.wait_ge(sums_full, use + 1)
                        nc.scalar.activation(small[:, 2 * a:2 * a + 2, :], sums_b[b][:].rearrange("p (c f) -> p c f", c=2),
                                             ACT.Copy, scale=SLOPE).then_inc(small_made, 1)
                    if front is not None and a == 0:
                        elu_turned(back, front, 3)

            act.wait_ge(dve_ready, 1)
            steps(act, step)

        @block.vector
        def _(dve):
            settled = [0]

            def settle(instruction):
                settled[0] = settled[0] + 1
                instruction.then_inc(dve_settled, 1)
                dve.wait_ge(dve_settled, settled[0])

            nc.vector.memset(minus_one[:], -1.0)
            nc.vector.memset(ones[:], 1.0)
            for sc in (sc1, sc2, sc3):
                nc.vector.memset(sc.cols[:], 0.0)
                nc.vector.memset(sc.diag[:], 0.0)
                nc.vector.memset(sc.split[:].bitcast(F32), 0.0)
            dve.wait_ge(pool_consts, 1)
            nc.vector.tensor_copy(ident_b[:], ident[:])
            dve.wait_ge(w_loaded, 16 * 12)
            for t in range(2):
                for g in range(2):
                    part = expo[:, 0:KC, 0:256]
                    settle(nc.vector.tensor_tensor(part, w1[:, :, g, 0:256],
                                                   att1[:, t, None, g * 256:g * 256 + 256].to_broadcast([P, KC, 256]),
                                                   ALU.mult))
                    settle(nc.vector.tensor_reduce(w1[:, :, g, 256 + 2 * t:258 + 2 * t],
                                                   part.rearrange("p c (h f) -> p c h f", h=2), AX.X, ALU.add))
                for w, att, n in ((w2, att2, NC), (w3, att3, KC)):
                    part = expo[:, 0:n, 0:DIM]
                    settle(nc.vector.tensor_tensor(part, w[:, :, 0:DIM], att[:, t, None, :].to_broadcast([P, n, DIM]),
                                                   ALU.mult))
                    settle(nc.vector.tensor_reduce(w[:, :, DIM + t:DIM + t + 1], part, AX.X, ALU.add))
            nc.vector.tensor_scalar(bias1[:], bias1[:], 1.0, None, ALU.add).then_inc(dve_ready, 1)
            start = settled[0]

            def half_moments(norm, src):
                for c in range(NC):
                    last = nc.vector.bn_stats(norm.halves[:, c, :], src[:, c, :])
                settle(last)

            def moments(which, norm):
                for c in range(NC):
                    last = nc.vector.bn_aggr(norm.stats[:, c, :], norm.halves[:, c, :])
                last.then_inc(var_made[which], 1)

            def normalise(b, which, norm, src):
                dve.wait_ge(rstd_made[which], b.n + 1)
                for c in range(NC):
                    last = nc.vector.tensor_scalar(norm.out[:, c, :], src[:, c, :], norm.stats[:, c, 0:1],
                                                   norm.rstd[:, c:c + 1], ALU.subtract, ALU.mult)
                last.then_inc(hn_made[which], 1)

            def rows_of(back, front, b, name, which, sc):
                use, k = ROWS.use(back, front, "rows" + name, 0)
                dve.wait_ge(rows_full, use + 1)
                h = sc.heads
                settle(nc.vector.tensor_reduce(sc.neg[0:h, :], rows_b[k][0:h, :], AX.X, ALU.max, negate=True))
                nc.vector.tensor_scalar(sc.diag[0:h, 0:h], ident[0:h, 0:h], sc.neg[0:h, :], None, ALU.mult
                                        ).then_inc(diag_made[which], 1)
                if which < 2:
                    settle(nc.vector.tensor_copy(sc.neg[32:32 + h, :], sc.neg[0:h, :]))
                    nc.vector.tensor_scalar(sc.row[32:32 + h, :], rows_b[k][32:32 + h, :], sc.neg[32:32 + h, :], 0.0,
                                            ALU.subtract, ALU.max).then_inc(rows_free, 1)
                else:
                    nc.vector.tensor_scalar(sc.row[0:h, :], rows_b[k][0:h, :], sc.neg[0:h, :], None, ALU.add
                                            ).then_inc(rows_free, 1)
                    dve.wait_ge(rows_free, use + 1)

            def split(b, which, sc):
                h = sc.heads
                if which < 2:
                    dve.wait_ge(q_made[which], b.n + 1)
                    whole, hi, lo = sc.q, 32, 0
                else:
                    whole, hi, lo = sc.row, 0, 32
                settle(nc.vector.tensor_copy(sc.split[hi:hi + h, :], whole[hi:hi + h, :]))
                nc.vector.tensor_tensor(sc.split[lo:lo + h, :], whole[hi:hi + h, :], sc.split[hi:hi + h, :].bitcast(F32),
                                        ALU.subtract).then_inc(split_made[which], 1)

            def shifted(back, front, b, name, which, sc):
                use, k = ROWS.use(back, front, "shift" + name, 0)
                dve.wait_ge(rows_full, use + 1)
                h = sc.heads
                nc.vector.tensor_tensor(sc.rel[:], sc.cols[:, :, 0:h],
                                        rows_b[k][:, None, 0:h].to_broadcast([P, NC, h]), ALU.add
                                        ).then_inc(rows_free, 1)

            def weights(back, front, b, name, i, which, sc, chunks=range(NC)):
                row, k = ROWS.use(back, front, "q" + name, i)
                use, s = PROB.use(back, front, "p" + name, i)
                if chunks[0] == 0:
                    dve.wait_ge(rows_full, row + 1)
                    dve.wait_ge(r_made[which], b.n + 1)
                for c in chunks:
                    last = nc.vector.scalar_tensor_tensor(out=prob[s][:, c, :], in0=rows_b[k][:],
                                                          scalar=sc.r[:, c, i:i + 1], in1=mask[b.slot][:, c, :],
                                                          op0=ALU.max, op1=ALU.mult)
                    last.then_inc(prob_full, 1)
                if chunks[-1] == NC - 1:
                    nc.vector.engine_nop().then_inc(rows_free, 1)

            def head_out(back, front, h):
                for a in range(2):
                    use, k = SUMS.use(back, front, "sum1", 2 * h + a)
                    dve.wait_ge(sums_full, use + 1)
                    S = sums_b[k][:, 0:258].rearrange("p (c f) -> p c f", c=2)
                    settle(nc.vector.reciprocal(rz1[:, 2 * h + a, :], S[:, :, HEAD_DIM]))
                    for c in range(2):
                        last = nc.vector.scalar_tensor_tensor(
                            out=z1[h % 2][:, 2 * a + c, :], in0=S[:, c, 0:HEAD_DIM], scalar=rz1[:, 2 * h + a, c:c + 1],
                            in1=bias1[:, h * HEAD_DIM:(h + 1) * HEAD_DIM], op0=ALU.mult, op1=ALU.add)
                    last.then_inc(sums_free, 1)

            def elu_out(back, front, h):
                n = front.n * HEADS + h
                dve.wait_ge(ez_made, n + 1)
                if h >= 2:
                    use, _ = TURN.use(back, front, "elu", h - 2)
                    dve.wait_ge(turn_full, use + 1)
                nc.vector.scalar_tensor_tensor(out=elu[h % 2][:], in0=ez[h % 2][:], scalar=1.0, in1=z1[h % 2][:],
                                               op0=ALU.min, op1=ALU.max).then_inc(elu_made, 1)

            def layer_out(back, front, c):
                use, k = SUMS.use(back, front, "sum2", c)
                dve.wait_ge(sums_full, use + 1)
                if c == 0 and back.after(1):
                    dve.wait_ge(out_made, back.n)
                settle(nc.vector.reciprocal(rz2[:, c:c + 1], sums_b[k][:, DIM:DIM + 1]))
                nc.vector.scalar_tensor_tensor(out=x1[:, c, :], in0=sums_b[k][:, 0:DIM], scalar=rz2[:, c:c + 1],
                                               in1=xb[back.slot][:, c, :], op0=ALU.mult, op1=ALU.add
                                               ).then_inc(sums_free, 1)

            def columns(back, front, name, last_use, which, sc):
                use, _ = PROJ.use(back, front, "proj" + name, last_use)
                dve.wait_ge(proj_free, use + 1)

            def step(back, front):
                if back is not None:
                    settled[0] = start + SETTLED_FRONT + back.n * (SETTLED_FRONT + SETTLED_BACK)
                begun = settled[0]
                if front is not None:
                    s = front.slot
                    dve.wait_ge(x_loaded[s], front.half * 16 + 16)
                    half_moments(norm1, x_in[s])
                    dve.wait_ge(adj_loaded[s], front.half * 16 + 16)
                    nc.vector.tensor_scalar(mask[s][:], adj_in[s][:], 0, None, ALU.is_gt).then_inc(mask_made, 1)
                    moments(0, norm1)
                    normalise(front, 0, norm1, x_in[s])
                if back is not None:
                    columns(back, front, "2", NC - 1, 1, sc2)
                    nc.vector.tensor_copy(sc2.cols[:, :, 0:1], xl2[:, :, DIM:DIM + 1])
                    nc.vector.tensor_copy(sc2.cols[:, :, 32:33], xl2[:, :, DIM + 1:DIM + 2]).then_inc(cols_made[1], 1)
                    rows_of(back, front, back, "2", 1, sc2)
                if front is not None:
                    use, _ = TURN.use(back, front, "mask", 1)
                    dve.wait_ge(turn_full, use + 1)
                    for c in range(NC):
                        own = mask[front.slot][:, c, c * P:(c + 1) * P]
                        nc.vector.tensor_tensor(own, own, ident_b[:], ALU.max)
                if back is not None:
                    split(back, 1, sc2)
                    shifted(back, front, back, "2", 1, sc2)
                    weights(back, front, back, "2", 0, 1, sc2)
                if front is not None:
                    columns(back, front, "1", 2 * NC - 1, 0, sc1)
                    for g in range(2):
                        nc.vector.tensor_copy(sc1.cols[:, :, 2 * g:2 * g + 2], xl1[:, :, g, 256:258])
                        last = nc.vector.tensor_copy(sc1.cols[:, :, 32 + 2 * g:34 + 2 * g], xl1[:, :, g, 258:260])
                    last.then_inc(cols_made[0], 1)
                if back is not None:
                    layer_out(back, front, 0)
                if front is not None:
                    rows_of(back, front, front, "1", 0, sc1)
                if back is not None:
                    layer_out(back, front, 1)
                if front is not None:
                    split(front, 0, sc1)
                    shifted(back, front, front, "1", 0, sc1)
                if back is not None:
                    layer_out(back, front, 2)
                if front is not None:
                    weights(back, front, front, "1", 0, 0, sc1, range(0, 2))
                if back is not None:
                    layer_out(back, front, 3)
                    use, _ = SUMS.use(back, front, "sum2", NC - 1)
                    dve.wait_ge(sums_free, use + 1)
                    half_moments(norm2, x1)
                if front is not None:
                    weights(back, front, front, "1", 0, 0, sc1, range(2, 4))
                if back is not None:
                    moments(1, norm2)
                if front is not None:
                    weights(back, front, front, "1", 1, 0, sc1)
                if back is not None:
                    normalise(back, 1, norm2, x1)
                if front is not None:
                    head_out(back, front, 0)
                    weights(back, front, front, "1", 2, 0, sc1, range(0, 2))
                    elu_out(back, front, 0)
                    weights(back, front, front, "1", 2, 0, sc1, range(2, 4))
                    head_out(back, front, 1)
                    weights(back, front, front, "1", 3, 0, sc1, range(0, 2))
                    elu_out(back, front, 1)
                    weights(back, front, front, "1", 3, 0, sc1, range(2, 4))
                if back is not None:
                    columns(back, front, "3", NC - 1, 2, sc3)
                    nc.vector.tensor_copy(sc3.cols[:, :, 0:1], xl3[:, :, DIM:DIM + 1])
                    nc.vector.tensor_copy(sc3.cols[:, :, 32:33], xl3[:, :, DIM + 1:DIM + 2]).then_inc(cols_made[2], 1)
                    rows_of(back, front, back, "3", 2, sc3)
                    split(back, 2, sc3)
                    use, k = ROWS.use(back, front, "shift3", 0)
                    dve.wait_ge(rows_full, use + 1)
                    nc.vector.tensor_scalar(low_col[:], sc3.cols[:, :, 32], rows_b[k][:, 0:1], 0.0,
                                            ALU.subtract, ALU.max).then_inc(rows_free, 1)
                    dve.wait_ge(rows_free, use + 1)
                    nc.vector.tensor_scalar(keep[:], count[back.slot][:], 1.0, None, ALU.min)
                    settle(nc.vector.tensor_scalar(low_col[:], low_col[:], -FALL, None, ALU.mult))
                    settle(nc.vector.tensor_scalar(empty[:], keep[:], -1.0, 1.0, ALU.mult, ALU.add))
                if front is not None:
                    head_out(back, front, 2)
                if back is not None:
                    use, k = ROWS.use(back, front, "q3", 0)
                    dve.wait_ge(low_row_made, back.n + 1)
                    for c in range(NC):
                        nc.vector.scalar_tensor_tensor(out=expo[:, c, :], in0=low_row[:], scalar=low_col[:, c:c + 1],
                                                       in1=rows_b[k][:], op0=ALU.add, op1=ALU.max
                                                       ).then_inc(expo_made, 1)
                    nc.vector.engine_nop().then_inc(rows_free, 1)
                if front is not None:
                    elu_out(back, front, 2)
                if back is not None:
                    use, s = PROB.use(back, front, "p3", 0)
                    for c in range(NC):
                        dve.wait_ge(e3_made, back.n * NC + (c + 1))
                        nc.vector.scalar_tensor_tensor(out=prob[s][:, c, :], in0=maskT[back.slot][:, c, :],
                                                       scalar=empty[:, c:c + 1], in1=expo[:, c, :], op0=ALU.max,
                                                       op1=ALU.mult, accum_out=z3[:, c:c + 1]).then_inc(prob_full, 1)
                        dve.wait_ge(prob_full, use * NC + (c + 1))
                        nc.vector.reciprocal(rz3[:, c:c + 1], z3[:, c:c + 1]).then_inc(rz3_made, 1)
                if front is not None:
                    head_out(back, front, 3)
                    elu_out(back, front, 3)
                if back is not None:
                    for a in range(2):
                        use, k = SUMS.use(back, front, "sum3", a)
                        dve.wait_ge(small_made, back.n * 2 + (a + 1))
                        nc.vector.tensor_tensor(small[:, 2 * a:2 * a + 2, :], small[:, 2 * a:2 * a + 2, :],
                                                sums_b[k][:].rearrange("p (c f) -> p c f", c=2), ALU.max
                                                ).then_inc(sums_free, 1)
                assert not isinstance(begun, int) or settled[0] - begun == (
                    SETTLED_FRONT * (front is not None) + SETTLED_BACK * (back is not None))

            steps(dve, step)

        @block.tensor
        def _(pe):
            def turn_bank(back, front, name, i):
                use, b = TURN.use(back, front, name, i)
                if older(use):
                    pe.wait_ge(turn_free, use - 1)
                return turn_b[b]

            def rows_bank(back, front, name, i=0):
                use, b = ROWS.use(back, front, name, i)
                if older(use):
                    pe.wait_ge(rows_free, use - 1)
                return rows_b[b]

            def turn_nodes(back, front, b, name, which, norm):
                pe.wait_ge(hn_made[which], b.n + 1)
                for k in range(KC):
                    T = turn_bank(back, front, name, k)
                    for c in range(NC):
                        last = nc.tensor.transpose(T[:, c * P:(c + 1) * P], norm.out[:, c, k * P:(k + 1) * P], ident[:])
                    last.then_inc(turn_full, 1)

            def project(back, front, name, i, lhs, w):
                use, b = PROJ.use(back, front, name, i)
                if older(use):
                    pe.wait_ge(proj_free, use - 1)
                n = w[0].shape[-1]
                for k in range(len(lhs)):
                    last = nc.tensor.matmul(proj_b[b][:, 0:n], lhs[k], w[k], start=(k == 0), stop=(k == len(lhs) - 1))
                last.then_inc(proj_full, 1)

            def rows(back, front, b, name, which, sc):
                pe.wait_ge(cols_made[which], b.n + 1)
                R = rows_bank(back, front, "rows" + name)
                for c in range(NC):
                    last = nc.tensor.transpose(R[:, c * P:(c + 1) * P], sc.cols[:, c, :], ident[:])
                last.then_inc(rows_full, 1)

            def shift(back, front, b, name, which, sc):
                pe.wait_ge(diag_made[which], b.n + 1)
                R = rows_bank(back, front, "shift" + name)
                nc.tensor.matmul(R[:, 0:sc.heads], ones[:], sc.diag[:, 0:sc.heads], start=True, stop=True
                                 ).then_inc(rows_full, 1)

            def spread_row(back, front, b, name, i, which, sc):
                pe.wait_ge(split_made[which], b.n + 1)
                R = rows_bank(back, front, "q" + name, i)
                nc.tensor.matmul(R[:], pick[:, i, :], sc.split[:], start=True, stop=True).then_inc(rows_full, 1)

            def weigh(back, front, name, i, p_name, p_i, chunks, n, y, first):
                use, k = SUMS.use(back, front, name, i)
                p_use, s = PROB.use(back, front, p_name, p_i)
                if older(use):
                    pe.wait_ge(sums_free, use - 1)
                for j, d in enumerate(chunks):
                    for c in range(NC):
                        if first and j == 0:
                            pe.wait_ge(prob_full, p_use * NC + (c + 1))
                        last = nc.tensor.matmul(sums_b[k][:, j * n:(j + 1) * n], prob[s][:, c, d * P:(d + 1) * P], y(c),
                                                start=(c == 0), stop=(c == NC - 1))
                last.then_inc(sums_full, 1)

            def head(back, front, h, a):
                if a == 0:
                    pe.wait_ge(y1_made, front.n * HEADS + (h + 1))
                weigh(back, front, "sum1", 2 * h + a, "p1", h, (2 * a, 2 * a + 1), HEAD_DIM + 1,
                      lambda c: y1[:, c, h, :], a == 0)

            def turn_elu(back, front, h):
                n = front.n * HEADS + h
                pe.wait_ge(elu_made, n + 1)
                T = turn_bank(back, front, "elu", h)
                for c in range(NC):
                    last = nc.tensor.transpose(T[:, c * P:(c + 1) * P], elu[h % 2][:, c, :], ident[:])
                last.then_inc(turn_full, 1)

            def proj1(back, front, c):
                for g in range(2):
                    project(back, front, "proj1", 2 * c + g, [norm1.T[:, k, c * P:(c + 1) * P] for k in range(KC)],
                            [w1[:, k, g, :] for k in range(KC)])

            def sum2(back, front, d):
                if d == 0:
                    pe.wait_ge(y2_made, back.n * NC + NC)
                weigh(back, front, "sum2", d, "p2", 0, (d,), DIM + 1, lambda c: y2[:, c, :], d == 0)

            def sum3(back, front, a):
                if a == 0:
                    pe.wait_ge(y3_made, back.n * NC + NC)
                weigh(back, front, "sum3", a, "p3", 0, (2 * a, 2 * a + 1), DIM, lambda c: y3[:, c, :], a == 0)

            def step(back, front):
                if back is not None:
                    pe.wait_ge(turn_free, back.n * TURN.whole + TURN.front)
                    for c in range(NC):
                        project(back, front, "proj2", c, [h2T[:, k, c * P:(c + 1) * P] for k in range(HEADS)],
                                [w2[:, k, :] for k in range(HEADS)])
                if front is not None:
                    turn_nodes(back, front, front, "hn1", 0, norm1)
                    pe.wait_ge(mask_made, front.n + 1)
                    for j in range(2):
                        T = turn_bank(back, front, "mask", j)[:].bitcast(BF16)
                        for k in range(2):
                            for c in range(NC):
                                at = k * NODES + c * P
                                last = nc.tensor.transpose(T[:, at:at + P],
                                                           mask[front.slot][:, c, (2 * j + k) * P:(2 * j + k + 1) * P],
                                                           ident_b[:])
                        last.then_inc(turn_full, 1)
                if back is not None:
                    rows(back, front, back, "2", 1, sc2)
                if front is not None:
                    use, _ = TURN.use(back, front, "hn1", KC - 1)
                    pe.wait_ge(turn_free, use + 1)
                    proj1(back, front, 0)
                    proj1(back, front, 1)
                if back is not None:
                    shift(back, front, back, "2", 1, sc2)
                if front is not None:
                    proj1(back, front, 2)
                if back is not None:
                    spread_row(back, front, back, "2", 0, 1, sc2)
                if front is not None:
                    proj1(back, front, 3)
                if back is not None:
                    sum2(back, front, 0)
                if front is not None:
                    rows(back, front, front, "1", 0, sc1)
                if back is not None:
                    sum2(back, front, 1)
                if front is not None:
                    shift(back, front, front, "1", 0, sc1)
                if back is not None:
                    sum2(back, front, 2)
                if front is not None:
                    spread_row(back, front, front, "1", 0, 0, sc1)
                if back is not None:
                    sum2(back, front, 3)
                if front is not None:
                    spread_row(back, front, front, "1", 1, 0, sc1)
                    head(back, front, 0, 0)
                    head(back, front, 0, 1)
                    spread_row(back, front, front, "1", 2, 0, sc1)
                    head(back, front, 1, 0)
                    head(back, front, 1, 1)
                if back is not None:
                    turn_nodes(back, front, back, "hn2", 1, norm2)
                if front is not None:
                    turn_elu(back, front, 0)
                if back is not None:
                    use, _ = TURN.use(back, front, "hn2", KC - 1)
                    pe.wait_ge(turn_free, use + 1)
                    for c in range(NC):
                        project(back, front, "proj3", c, [norm2.T[:, k, c * P:(c + 1) * P] for k in range(KC)],
                                [w3[:, k, :] for k in range(KC)])
                if front is not None:
                    spread_row(back, front, front, "1", 3, 0, sc1)
                    head(back, front, 2, 0)
                if back is not None:
                    rows(back, front, back, "3", 2, sc3)
                if front is not None:
                    turn_elu(back, front, 1)
                    head(back, front, 2, 1)
                if back is not None:
                    shift(back, front, back, "3", 2, sc3)
                if front is not None:
                    head(back, front, 3, 0)
                if back is not None:
                    spread_row(back, front, back, "3", 0, 2, sc3)
                if front is not None:
                    head(back, front, 3, 1)
                    turn_elu(back, front, 2)
                if back is not None:
                    sum3(back, front, 0)
                if front is not None:
                    turn_elu(back, front, 3)
                if back is not None:
                    sum3(back, front, 1)

            pe.wait_ge(dve_ready, 1)
            pe.wait_ge(pool_consts, 2)
            steps(pe, step)


_INS = ["x", "adj", "L0_gnn_W1", "L0_gnn_att_src1", "L0_gnn_att_dst1", "L0_gnn_b1", "L0_gnn_W2",
        "L0_gnn_att_src2", "L0_gnn_att_dst2", "L0_gnn_b2", "L1_gnn_W", "L1_gnn_a"]


def kernel(**inputs):
    import numpy as _np
    import concourse.bacc as _bacc
    from concourse import mybir as _mybir
    from concourse.bass_utils import run_bass_kernel_spmd as _run

    nc = _bacc.Bacc("TRN2", target_bir_lowering=False, num_devices=1)
    arrays, args = {}, []
    for name in _INS:
        a = _np.ascontiguousarray(inputs[name])
        arrays[f"in_{name}"] = a
        args.append(nc.dram_tensor(f"in_{name}", a.shape, _mybir.dt.from_np(a.dtype), kind="ExternalInput").ap())
    out = nc.dram_tensor("out_x", (BATCHES, NODES, DIM), F32, kind="ExternalOutput").ap()
    gat_block(nc, *args, out)
    r = _run(nc, [arrays], core_ids=[0])
    return r.results[0]["out_x"]
```

```python
from contextlib import ExitStack
from typing import NamedTuple

import concourse.bass as bass
from concourse import mybir

P = 128
F32 = mybir.dt.float32
F32R = mybir.dt.float32r
BF16 = mybir.dt.bfloat16
I32 = mybir.dt.int32
ALU = mybir.AluOpType
ACT = mybir.ActivationFunctionType
AX = mybir.AxisListType

BATCHES = 16
NODES = 512
DIM = 256
HEADS = 4
HEAD_DIM = 128
WIDE = HEADS * HEAD_DIM
NC = NODES // P
KC = DIM // P
EPS = 1e-5
SETTLED = {"after": 1, "front": 10, "back": 12, "tail": 2}
SLOPE = 0.2
FALL = 1.0 - SLOPE


GRAPHS = {"after": -1, "front": 0, "back": 1, "tail": 2}


class Graph(NamedTuple):
    n: object
    half: object
    slot: int


class Step:

    def __init__(self, t, even=None):
        self.t = t if even is None else even * 2 + (2 + t)
        self.looped = even is not None
        self.parity = t % 2

        def graph(back):
            if even is None:
                n = t - back
                return Graph(n, n // 2, n % 2) if 0 <= n < BATCHES else None
            m = 2 + t - back
            return Graph(even * 2 + m, even + m // 2, m % 2)

        self.after, self.front, self.back, self.tail = graph(-1), graph(0), graph(1), graph(2)

    def has(self, graph):
        return {"after": self.after, "front": self.front, "back": self.back, "tail": self.tail}[graph] is not None


def count_before(s, of):
    if s.looped:
        return s.t * sum(of.values()) + (of["after"] - of["back"] - 2 * of["tail"])
    return sum(of[g] * min(max(s.t - late, 0), BATCHES) for g, late in GRAPHS.items())


class Ring:

    def __init__(self, *order):
        self.order = order
        self.of = {g: sum(c for _, graph, c in order if graph == g) for g in GRAPHS}
        assert sum(self.of.values()) % 2 == 0

    def before(self, s):
        n = count_before(s, self.of)
        return n, (self.of["after"] + self.of["back"]) % 2 if s.looped else n % 2

    def use(self, s, name, i=0):
        at = i
        for what, graph, count in self.order:
            if what == name:
                break
            if s.has(graph):
                at += count
        base, odd = self.before(s)
        return base + at, (odd + at) % 2

    def last(self, s, back):
        base, odd = self.before(s)
        return base - back, (odd + back) % 2


def older(use):
    return not isinstance(use, int) or use >= 2


TURN = Ring(("elu3", "back", 1), ("mask", "front", 2), ("elu0", "front", 1),
            ("hn2", "back", KC), ("elu1", "front", 1), ("hn1", "after", KC), ("elu2", "front", 1))
PROJ = Ring(("proj1", "front", 2 * NC), ("proj2", "back", NC), ("proj3", "back", NC))
SUMS = Ring(("sum3", "tail", 2), ("head0", "front", 2), ("sum2", "back", NC), ("head1", "front", 2),
            ("head2", "front", 2), ("head3", "front", 2))
ROWS = Ring(("shift3", "tail", 1), ("q3", "tail", 1), ("rows1", "front", 1), ("shift1", "front", 1),
            ("q1_0", "front", 1), ("rows2", "back", 1), ("shift2", "back", 1), ("q2", "back", 1),
            ("q1_1", "front", 1), ("q1_2", "front", 1), ("q1_3", "front", 1), ("rows3", "back", 1))


def steps(engine, step):
    for t in range(-1, 2):
        step(Step(t))
    with engine.Fori(0, (BATCHES - 4) // 2) as i:
        for t in range(2):
            step(Step(t, i))
    for t in range(BATCHES - 2, BATCHES + 2):
        step(Step(t))


def gat_block(nc, x, adj, W1, src1, dst1, b1, W2, src2, dst2, b2, W3, a3, out):
    with ExitStack() as ctx:
        def sb(name, shape, dt=F32):
            return ctx.enter_context(nc.sbuf_tensor(name, shape, dt))

        def bank(name):
            return ctx.enter_context(nc.psum_tensor(name, [P, 512], F32))

        def sem(name):
            return ctx.enter_context(nc.semaphore(name))

        ident = sb("ident", [P, P])
        ident_b = sb("ident_b", [P, P], BF16)
        ones = sb("ones", [P, P])
        pick = sb("pick", [P, HEADS, P], F32R)
        w1 = sb("w1", [P, KC, 2, 260])
        w2 = sb("w2", [P, NC, DIM + 2])
        w3 = sb("w3", [P, KC, DIM + 2])
        bias1 = sb("bias1", [P, WIDE])
        bias2 = sb("bias2", [P, DIM])
        minus_one = sb("minus_one", [P, 1])
        eps = sb("eps", [P, NC])
        half_power = sb("half_power", [P, NC])

        x_in = [sb(f"x_in{s}", [P, NC, DIM]) for s in range(2)]
        adj_in = [sb(f"adj_in{s}", [P, NC, NODES], I32) for s in range(2)]
        xb = [sb(f"xb{s}", [P, NC, DIM]) for s in range(2)]
        mask = [sb(f"mask{s}", [P, NC, NODES], BF16) for s in range(2)]
        maskT = [sb(f"maskT{s}", [P, NC, NODES], BF16) for s in range(2)]
        count = [sb(f"count{s}", [P, NC]) for s in range(2)]
        keep = sb("keep", [P, NC])
        empty = sb("empty", [P, NC])

        class Norm:
            def __init__(self, name):
                self.halves = sb(f"halves_{name}", [P, NC, 6])
                self.stats = sb(f"stats_{name}", [P, NC, 2])
                self.var = sb(f"var_{name}", [P, NC])
                self.rstd = sb(f"rstd_{name}", [P, NC])
                self.out = sb(f"hn_{name}", [P, NC, DIM])
                self.T = sb(f"hT_{name}", [P, KC, NODES])

        norm1, norm2 = Norm("1"), Norm("2")

        class Scores:
            def __init__(self, name, heads):
                self.heads = heads
                self.cols = sb(f"cols_{name}", [P, NC, P])
                self.neg = sb(f"neg_{name}", [P, 1])
                self.diag = sb(f"diag_{name}", [P, HEADS])
                self.row = sb(f"row_{name}", [P, NODES])
                self.q = sb(f"q_{name}", [P, NODES]) if name != "3" else None
                self.split = sb(f"split_{name}", [P, NODES], F32R)
                self.rel = sb(f"rel_{name}", [P, NC, heads])
                self.r = sb(f"r_{name}", [P, NC, heads])

        sc1, sc2, sc3 = Scores("1", HEADS), Scores("2", 1), Scores("3", 1)
        xl1 = sb("xl1", [P, NC, 2, 260])
        y1 = sb("y1", [P, NC, HEADS, HEAD_DIM + 1])
        xl2 = sb("xl2", [P, NC, DIM + 2])
        y2 = sb("y2", [P, NC, DIM + 1])
        xl3 = sb("xl3", [P, NC, DIM + 2])
        y3 = sb("y3", [P, NC, DIM])
        prob1 = [sb(f"prob1_{s}", [P, NC, NODES]) for s in range(2)]
        prob2 = sb("prob2", [P, NC, NODES])
        prob3 = sb("prob3", [P, NC, NODES])
        rz1 = sb("rz1", [P, 2 * HEADS, 2])
        z1 = [sb(f"z1_{s}", [P, NC, HEAD_DIM]) for s in range(2)]
        ez = [sb(f"ez_{s}", [P, NC, HEAD_DIM]) for s in range(2)]
        elu = [sb(f"elu_{s}", [P, NC, HEAD_DIM]) for s in range(2)]
        h2T = sb("h2T", [P, HEADS, NODES])
        rz2 = sb("rz2", [P, NC])
        low_row = sb("low_row", [P, NODES])
        low_col = sb("low_col", [P, NC])
        expo = sb("expo", [P, NC, NODES])
        z3 = sb("z3", [P, NC])
        rz3 = sb("rz3", [P, NC])
        small = sb("small", [P, NC, DIM])
        o = sb("o", [P, NC, DIM])
        att1 = o[:].rearrange("p c f -> p (c f)").rearrange("p (t n) -> p t n", t=2)
        att2, att3 = small[:, 0:2, :], small[:, 2:4, :]
        pick_f = low_row[:].rearrange("p (h m) -> p h m", h=HEADS)

        turn_b = [bank(f"turn{i}") for i in range(2)]
        proj_b = [bank(f"proj{i}") for i in range(2)]
        sums_b = [bank(f"sums{i}") for i in range(2)]
        rows_b = [bank(f"rows{i}") for i in range(2)]

        w1_loaded = sem("w1_loaded")
        w_loaded = sem("w_loaded")
        x_loaded = [sem(f"x_loaded{s}") for s in range(2)]
        adj_loaded = [sem(f"adj_loaded{s}") for s in range(2)]
        out_stored = sem("out_stored")
        pool_consts = sem("pool_consts")
        w1_ready = sem("w1_ready")
        w_ready = sem("w_ready")
        w_settled = sem("w_settled")
        dve_settled = sem("dve_settled")
        pool_settled = sem("pool_settled")
        eps_added = [sem(f"eps_added{i}") for i in range(2)]
        mask_made = sem("mask_made")
        xb_made = sem("xb_made")
        var_made = [sem(f"var_made{i}") for i in range(2)]
        rstd_made = [sem(f"rstd_made{i}") for i in range(2)]
        hn_made = [sem(f"hn_made{i}") for i in range(2)]
        turn_full, turn_free = sem("turn_full"), sem("turn_free")
        proj_full, proj_free = sem("proj_full"), sem("proj_free")
        sums_full, sums_free = sem("sums_full"), sem("sums_free")
        rows_full, rows_free = sem("rows_full"), sem("rows_free")
        prob_full = [sem(f"prob_full{i}") for i in range(3)]
        cols_made = [sem(f"cols_made{i}") for i in range(3)]
        diag_made = [sem(f"diag_made{i}") for i in range(3)]
        q_made = [sem(f"q_made{i}") for i in range(2)]
        split_made = [sem(f"split_made{i}") for i in range(3)]
        r_made = [sem(f"r_made{i}") for i in range(2)]
        y1_made = sem("y1_made")
        y2_made = sem("y2_made")
        y3_made = sem("y3_made")
        ez_made = sem("ez_made")
        elu_made = sem("elu_made")
        low_row_made = sem("low_row_made")
        expo_made = sem("expo_made")
        e3_made = sem("e3_made")
        rz3_made = sem("rz3_made")
        small_made = sem("small_made")
        out_made = sem("out_made")

        x_v = x.rearrange("b (c p) d -> b p c d", p=P)
        adj_v = adj.rearrange("b (c p) d -> b p c d", p=P)
        out_v = out.rearrange("b (c p) d -> b p c d", p=P)

        def spread(row):
            return row.to_broadcast([P, row.shape[1]])

        block = ctx.enter_context(nc.Block())

        @block.sync
        def _(sp):
            sp.dma_start(x_in[0][:], x_v[0]).then_inc(x_loaded[0], 16)
            for g in range(2):
                sp.dma_start(w1[:, :, g, 0:256], W1.rearrange("(c p) n -> p c n", p=P)[:, :, g * 256:g * 256 + 256]
                             ).then_inc(w1_loaded, 16)
            sp.dma_start(att1[:, 0, :], spread(src1.rearrange("(o h) f -> o (h f)", o=1))).then_inc(w1_loaded, 16)
            sp.dma_start(att1[:, 1, :], spread(dst1.rearrange("(o h) f -> o (h f)", o=1))).then_inc(w1_loaded, 16)
            sp.dma_start(adj_in[0][:], adj_v[0]).then_inc(adj_loaded[0], 16)
            sp.dma_start(w2[:, :, 0:DIM], W2.rearrange("(c p) n -> p c n", p=P)).then_inc(w_loaded, 16)
            sp.dma_start(att2[:, 0, :], spread(src2)).then_inc(w_loaded, 16)
            sp.dma_start(att2[:, 1, :], spread(dst2)).then_inc(w_loaded, 16)
            sp.dma_start(w3[:, :, 0:DIM], W3.rearrange("(c p) n -> p c n", p=P)).then_inc(w_loaded, 16)
            a3_v = a3.rearrange("(t f) o -> t (f o)", t=2)
            sp.dma_start(att3[:, 0, :], spread(a3_v[0:1, :])).then_inc(w_loaded, 16)
            sp.dma_start(att3[:, 1, :], spread(a3_v[1:2, :])).then_inc(w_loaded, 16)
            sp.dma_start(bias1[:], spread(b1.rearrange("(o n) -> o n", o=1))).then_inc(w_loaded, 16)
            sp.dma_start(bias2[:], spread(b2.rearrange("(o n) -> o n", o=1))).then_inc(w_loaded, 16)
            sp.dma_start(x_in[1][:], x_v[1]).then_inc(x_loaded[1], 16)
            sp.dma_start(adj_in[1][:], adj_v[1]).then_inc(adj_loaded[1], 16)

            def load(b):
                sp.wait_ge(xb_made, b.n + 1)
                sp.wait_ge(hn_made[0], b.n + 1)
                sp.dma_start(x_in[b.slot][:], x_v[b.n + 2]).then_inc(x_loaded[b.slot], 16)
                sp.wait_ge(mask_made, b.n + 1)
                sp.dma_start(adj_in[b.slot][:], adj_v[b.n + 2]).then_inc(adj_loaded[b.slot], 16)

            def store(n):
                sp.wait_ge(out_made, n + 1)
                sp.dma_start(out_v[n], o[:]).then_inc(out_stored, 16)

            load(Graph(0, 0, 0))
            with sp.Fori(0, (BATCHES - 4) // 2) as i:
                load(Graph(i * 2 + 1, i, 1))
                store(i * 2)
                load(Graph(i * 2 + 2, i + 1, 0))
                store(i * 2 + 1)
            load(Graph(BATCHES - 3, 0, 1))
            for n in range(BATCHES - 4, BATCHES):
                store(n)
            sp.wait_ge(out_stored, 16 * BATCHES)

        @block.gpsimd
        def _(pool):
            nc.gpsimd.memset(half_power[:], -0.5)
            nc.gpsimd.memset(eps[:], EPS)
            nc.gpsimd.memset(ident[:], 0.0).then_inc(pool_settled, 1)
            nc.gpsimd.memset(pick_f, 0.0).then_inc(pool_settled, 1)
            pool.wait_ge(pool_settled, 2)
            nc.gpsimd.affine_select(out=ident[:], in_=ident[:], compare_op=ALU.not_equal, fill=1.0, base=0,
                                    pattern=[[-1, P]], channel_multiplier=1).then_inc(pool_consts, 1)
            for lift in (0, 32):
                nc.gpsimd.affine_select(out=pick_f, in_=pick_f, compare_op=ALU.not_equal, fill=1.0, base=-lift,
                                        pattern=[[-1, HEADS], [0, P]], channel_multiplier=1).then_inc(pool_settled, 1)
                pool.wait_ge(pool_settled, 3 + lift // 32)
            nc.gpsimd.tensor_copy(pick[:], pick_f).then_inc(pool_consts, 1)

            def rstd(b, which, norm):
                pool.wait_ge(var_made[which], b.n + 1)
                nc.gpsimd.tensor_tensor(norm.var[:], norm.stats[:, :, 1], eps[:], ALU.add
                                        ).then_inc(eps_added[which], 1)
                pool.wait_ge(eps_added[which], b.n + 1)
                nc.gpsimd.tensor_tensor(norm.rstd[:], norm.var[:], half_power[:], ALU.pow
                                        ).then_inc(rstd_made[which], 1)

            def step(s):
                if s.front:
                    pool.wait_ge(r_made[0], s.front.n + 1)
                    for h in range(HEADS):
                        g, at = h // 2, h % 2 * HEAD_DIM
                        nc.gpsimd.tensor_tensor(
                            y1[:, :, h, 0:HEAD_DIM], xl1[:, :, g, at:at + HEAD_DIM],
                            y1[:, :, h, HEAD_DIM:HEAD_DIM + 1].to_broadcast([P, NC, HEAD_DIM]), ALU.mult
                        ).then_inc(y1_made, 1)
                if s.tail:
                    use, _ = SUMS.use(s, "sum3", 1)
                    pool.wait_ge(sums_free, use + 1)
                    if s.looped or s.tail.n > 0:
                        pool.wait_ge(out_stored, s.tail.n * 16)
                    nc.gpsimd.tensor_tensor(o[:], small[:], xb[s.tail.slot][:], ALU.add).then_inc(out_made, 1)
                if s.front:
                    if s.tail:
                        pool.wait_ge(out_made, s.tail.n + 1)
                    if not s.looped and s.t == 0:
                        pool.wait_ge(w_loaded, 16 * 8)
                    pool.wait_ge(x_loaded[s.front.slot], s.front.half * 16 + 16)
                    nc.gpsimd.tensor_tensor(xb[s.front.slot][:], x_in[s.front.slot][:],
                                            bias2[:, None, :].to_broadcast([P, NC, DIM]), ALU.add
                                            ).then_inc(xb_made, 1)
                if s.after:
                    rstd(s.after, 0, norm1)
                if s.back:
                    rstd(s.back, 1, norm2)

            steps(pool, step)

        @block.scalar
        def _(act):
            def from_proj(s, name, i, dst):
                use, b = PROJ.use(s, name, i)
                act.wait_ge(proj_full, use + 1)
                nc.scalar.copy(dst, proj_b[b][:, 0:dst.shape[-1]]).then_inc(proj_free, 1)

            def relu_turned(s, name, norm):
                for c in range(KC):
                    use, b = TURN.use(s, name, c)
                    act.wait_ge(turn_full, use + 1)
                    nc.scalar.activation(norm.T[:, c, :], turn_b[b][:], ACT.Relu).then_inc(turn_free, 1)

            def q_row(s, name, which, sc):
                use, _ = ROWS.use(s, "rows" + name)
                act.wait_ge(rows_free, use + 1)
                nc.scalar.activation(sc.q[32:32 + sc.heads, :], sc.row[32:32 + sc.heads, :], ACT.Exp, scale=-FALL
                                     ).then_inc(q_made[which], 1)

            def r_cols(s, name, which, sc, low):
                use, _ = ROWS.use(s, "shift" + name)
                act.wait_ge(rows_free, use + 1)
                nc.scalar.activation(sc.r[:], sc.rel[:], ACT.Exp, scale=FALL)
                nc.scalar.activation(low, sc.rel[:], ACT.Exp, scale=SLOPE).then_inc(r_made[which], 1)

            def elu_exp(h, use):
                act.wait_ge(sums_free, use + 1)
                nc.scalar.activation(ez[h % 2][:], z1[h % 2][:], ACT.Exp, bias=minus_one[:]).then_inc(ez_made, 1)

            def elu_turned(s, h):
                use, b = TURN.use(s, f"elu{h}")
                act.wait_ge(turn_full, use + 1)
                nc.scalar.activation(h2T[:, h, :], turn_b[b][:], ACT.Identity, bias=minus_one[:]
                                     ).then_inc(turn_free, 1)

            def low_sums(s, a):
                use, b = SUMS.use(s, "sum3", a)
                act.wait_ge(sums_full, use + 1)
                nc.scalar.activation(small[:, 2 * a:2 * a + 2, :], sums_b[b][:].rearrange("p (c f) -> p c f", c=2),
                                     ACT.Copy, scale=SLOPE).then_inc(small_made, 1)

            def mask_turned(s, j):
                use, b = TURN.use(s, "mask", j)
                act.wait_ge(turn_full, use + 1)
                for k in range(2):
                    c = 2 * j + k
                    last = nc.scalar.activation(maskT[s.front.slot][:, c, :],
                                                turn_b[b][:].bitcast(BF16)[:, k * NODES:(k + 1) * NODES], ACT.Copy,
                                                accum_out=count[s.front.slot][:, c:c + 1])
                last.then_inc(turn_free, 1)

            def exps3(s, c):
                act.wait_ge(expo_made, s.tail.n * NC + (c + 1))
                nc.scalar.activation(expo[:, c, :], expo[:, c, :], ACT.Exp, scale=keep[:, c:c + 1]).then_inc(e3_made, 1)

            def scale3(s, c):
                act.wait_ge(rz3_made, s.tail.n * NC + (c + 1))
                nc.scalar.activation(y3[:, c, :], xl3[:, c, 0:DIM], ACT.Copy, scale=rz3[:, c:c + 1]).then_inc(y3_made, 1)

            def proj1(s, c):
                for g in range(2):
                    from_proj(s, "proj1", 2 * c + g, xl1[:, c, g, :])

            def step(s):
                if s.front:
                    if s.looped or s.t != 0:
                        act.wait_ge(y1_made, s.front.n * HEADS)
                    proj1(s, 0)
                if s.tail:
                    use, b = ROWS.use(s, "q3")
                    act.wait_ge(rows_full, use + 1)
                    nc.scalar.activation(low_row[:], rows_b[b][:], ACT.Copy, scale=SLOPE).then_inc(low_row_made, 1)
                for c in range(1, NC):
                    if s.front:
                        proj1(s, c)
                    if c == 1 and s.back:
                        elu_exp(3, SUMS.last(s, 1)[0])
                    if s.tail:
                        exps3(s, c - 1)
                if s.back:
                    elu_turned(s, 3)
                if s.tail:
                    exps3(s, NC - 1)
                    scale3(s, 0)
                if s.back:
                    from_proj(s, "proj2", 0, xl2[:, 0, :])
                if s.tail:
                    scale3(s, 1)
                if s.front:
                    q_row(s, "1", 0, sc1)
                if s.back:
                    from_proj(s, "proj2", 1, xl2[:, 1, :])
                if s.tail:
                    scale3(s, 2)
                if s.back:
                    from_proj(s, "proj2", 2, xl2[:, 2, :])
                if s.tail:
                    scale3(s, 3)
                if s.front:
                    r_cols(s, "1", 0, sc1, y1[:, :, :, HEAD_DIM])
                if s.back:
                    from_proj(s, "proj2", 3, xl2[:, 3, :])
                if s.front:
                    mask_turned(s, 0)
                    mask_turned(s, 1)
                if s.back:
                    q_row(s, "2", 1, sc2)
                if s.tail:
                    low_sums(s, 0)
                if s.back:
                    r_cols(s, "2", 1, sc2, y2[:, :, DIM:DIM + 1])
                    act.wait_ge(r_made[1], s.back.n + 1)
                    for c in range(NC):
                        nc.scalar.activation(y2[:, c, 0:DIM], xl2[:, c, 0:DIM], ACT.Copy,
                                             scale=y2[:, c, DIM:DIM + 1]).then_inc(y2_made, 1)
                if s.tail:
                    low_sums(s, 1)
                if s.front:
                    elu_exp(0, SUMS.use(s, "head0", 1)[0])
                    elu_turned(s, 0)
                    elu_exp(1, SUMS.use(s, "head1", 1)[0])
                if s.back:
                    relu_turned(s, "hn2", norm2)
                if s.front:
                    elu_turned(s, 1)
                if s.back:
                    for c in range(NC):
                        from_proj(s, "proj3", c, xl3[:, c, :])
                if s.front:
                    elu_exp(2, SUMS.use(s, "head2", 1)[0])
                if s.after:
                    relu_turned(s, "hn1", norm1)
                if s.front:
                    elu_turned(s, 2)

            act.wait_ge(pool_consts, 1)
            nc.scalar.activation(rz2[:], eps[:], ACT.Exp)
            steps(act, step)

        @block.vector
        def _(dve):
            settled = [0]

            def settle(instruction):
                settled[0] = settled[0] + 1
                instruction.then_inc(dve_settled, 1)
                dve.wait_ge(dve_settled, settled[0])

            nc.vector.memset(minus_one[:], -1.0)
            nc.vector.memset(ones[:], 1.0)
            for sc in (sc1, sc2, sc3):
                nc.vector.memset(sc.cols[:], 0.0)
                nc.vector.memset(sc.diag[:], 0.0)
                nc.vector.memset(sc.split[:].bitcast(F32), 0.0)
            dve.wait_ge(pool_consts, 1)
            nc.vector.tensor_copy(ident_b[:], ident[:])
            prepared = [0]

            def weights_settle(instruction):
                prepared[0] += 1
                instruction.then_inc(w_settled, 1)
                dve.wait_ge(w_settled, prepared[0])

            def prepare_w1():
                dve.wait_ge(w1_loaded, 16 * 4)
                for t in range(2):
                    for g in range(2):
                        part = expo[:, 0:KC, 0:256]
                        weights_settle(nc.vector.tensor_tensor(
                            part, w1[:, :, g, 0:256],
                            att1[:, t, None, g * 256:g * 256 + 256].to_broadcast([P, KC, 256]), ALU.mult))
                        weights_settle(nc.vector.tensor_reduce(w1[:, :, g, 256 + 2 * t:258 + 2 * t],
                                                               part.rearrange("p c (h f) -> p c h f", h=2),
                                                               AX.X, ALU.add))
                nc.vector.engine_nop().then_inc(w1_ready, 1)

            def prepare_w2_w3():
                dve.wait_ge(w_loaded, 16 * 8)
                for t in range(2):
                    for w, att, n in ((w2, att2, NC), (w3, att3, KC)):
                        part = expo[:, 0:n, 0:DIM]
                        weights_settle(nc.vector.tensor_tensor(part, w[:, :, 0:DIM],
                                                               att[:, t, None, :].to_broadcast([P, n, DIM]), ALU.mult))
                        weights_settle(nc.vector.tensor_reduce(w[:, :, DIM + t:DIM + t + 1], part, AX.X, ALU.add))
                nc.vector.tensor_scalar(bias1[:], bias1[:], 1.0, None, ALU.add).then_inc(w_ready, 1)


            def half_moments(norm, src):
                for c in range(NC):
                    last = nc.vector.bn_stats(norm.halves[:, c, :], src[:, c, :])
                settle(last)

            def moments(which, norm):
                for c in range(NC):
                    last = nc.vector.bn_aggr(norm.stats[:, c, :], norm.halves[:, c, :])
                last.then_inc(var_made[which], 1)

            def normalise(b, which, norm, src):
                dve.wait_ge(rstd_made[which], b.n + 1)
                for c in range(NC):
                    last = nc.vector.tensor_scalar(norm.out[:, c, :], src[:, c, :], norm.stats[:, c, 0:1],
                                                   norm.rstd[:, c:c + 1], ALU.subtract, ALU.mult)
                last.then_inc(hn_made[which], 1)

            def rows_of(s, b, name, which, sc):
                use, k = ROWS.use(s, "rows" + name)
                dve.wait_ge(rows_full, use + 1)
                h = sc.heads
                settle(nc.vector.tensor_reduce(sc.neg[0:h, :], rows_b[k][0:h, :], AX.X, ALU.max, negate=True))
                nc.vector.tensor_scalar(sc.diag[0:h, 0:h], ident[0:h, 0:h], sc.neg[0:h, :], None, ALU.mult
                                        ).then_inc(diag_made[which], 1)
                if which < 2:
                    settle(nc.vector.tensor_copy(sc.neg[32:32 + h, :], sc.neg[0:h, :]))
                    nc.vector.tensor_scalar(sc.row[32:32 + h, :], rows_b[k][32:32 + h, :], sc.neg[32:32 + h, :], 0.0,
                                            ALU.subtract, ALU.max).then_inc(rows_free, 1)
                else:
                    nc.vector.tensor_scalar(sc.row[0:h, :], rows_b[k][0:h, :], sc.neg[0:h, :], None, ALU.add
                                            ).then_inc(rows_free, 1)
                    dve.wait_ge(rows_free, use + 1)

            def split(b, which, sc):
                h = sc.heads
                if which < 2:
                    dve.wait_ge(q_made[which], b.n + 1)
                    whole, hi, lo = sc.q, 32, 0
                else:
                    whole, hi, lo = sc.row, 0, 32
                settle(nc.vector.tensor_copy(sc.split[hi:hi + h, :], whole[hi:hi + h, :]))
                nc.vector.tensor_tensor(sc.split[lo:lo + h, :], whole[hi:hi + h, :], sc.split[hi:hi + h, :].bitcast(F32),
                                        ALU.subtract).then_inc(split_made[which], 1)

            def shifted(s, name, sc):
                use, k = ROWS.use(s, "shift" + name)
                dve.wait_ge(rows_full, use + 1)
                h = sc.heads
                nc.vector.tensor_tensor(sc.rel[:], sc.cols[:, :, 0:h],
                                        rows_b[k][:, None, 0:h].to_broadcast([P, NC, h]), ALU.add
                                        ).then_inc(rows_free, 1)

            def weights(s, b, name, i, which, sc, into, chunks=range(NC)):
                row, k = ROWS.use(s, name)
                if chunks[0] == 0:
                    dve.wait_ge(rows_full, row + 1)
                    dve.wait_ge(r_made[which], b.n + 1)
                for c in chunks:
                    nc.vector.scalar_tensor_tensor(out=into[:, c, :], in0=rows_b[k][:], scalar=sc.r[:, c, i:i + 1],
                                                   in1=mask[b.slot][:, c, :], op0=ALU.max, op1=ALU.mult
                                                   ).then_inc(prob_full[which], 1)
                if chunks[-1] == NC - 1:
                    nc.vector.engine_nop().then_inc(rows_free, 1)

            def head_weights(s, h, chunks=range(NC)):
                weights(s, s.front, f"q1_{h}", h, 0, sc1, prob1[h % 2], chunks)

            def head_out(h, uses):
                for a, (use, k) in enumerate(uses):
                    dve.wait_ge(sums_full, use + 1)
                    S = sums_b[k][:, 0:258].rearrange("p (c f) -> p c f", c=2)
                    settle(nc.vector.reciprocal(rz1[:, 2 * h + a, :], S[:, :, HEAD_DIM]))
                    for c in range(2):
                        last = nc.vector.scalar_tensor_tensor(
                            out=z1[h % 2][:, 2 * a + c, :], in0=S[:, c, 0:HEAD_DIM], scalar=rz1[:, 2 * h + a, c:c + 1],
                            in1=bias1[:, h * HEAD_DIM:(h + 1) * HEAD_DIM], op0=ALU.mult, op1=ALU.add)
                    last.then_inc(sums_free, 1)

            def elu_out(s, b, h):
                dve.wait_ge(ez_made, b.n * HEADS + (h + 1))
                if h == 2:
                    use, _ = TURN.use(s, "elu0")
                    dve.wait_ge(turn_full, use + 1)
                nc.vector.scalar_tensor_tensor(out=elu[h % 2][:], in0=ez[h % 2][:], scalar=1.0, in1=z1[h % 2][:],
                                               op0=ALU.min, op1=ALU.max).then_inc(elu_made, 1)

            def layer_out(s, c):
                use, k = SUMS.use(s, "sum2", c)
                dve.wait_ge(sums_full, use + 1)
                settle(nc.vector.reciprocal(rz2[:, c:c + 1], sums_b[k][:, DIM:DIM + 1]))
                if c == 0:
                    dve.wait_ge(xb_made, s.back.n + 1)
                x1 = xb[s.back.slot][:, c, :]
                nc.vector.scalar_tensor_tensor(out=x1, in0=sums_b[k][:, 0:DIM], scalar=rz2[:, c:c + 1],
                                               in1=x1, op0=ALU.mult, op1=ALU.add).then_inc(sums_free, 1)

            def weights3(s, c):
                n = s.tail.n * NC + (c + 1)
                dve.wait_ge(e3_made, n)
                nc.vector.scalar_tensor_tensor(out=prob3[:, c, :], in0=maskT[s.tail.slot][:, c, :],
                                               scalar=empty[:, c:c + 1], in1=expo[:, c, :], op0=ALU.max,
                                               op1=ALU.mult, accum_out=z3[:, c:c + 1]).then_inc(prob_full[2], 1)
                dve.wait_ge(prob_full[2], n)
                nc.vector.reciprocal(rz3[:, c:c + 1], z3[:, c:c + 1]).then_inc(rz3_made, 1)

            def leaky_sums(s, a):
                use, k = SUMS.use(s, "sum3", a)
                dve.wait_ge(small_made, s.tail.n * 2 + (a + 1))
                nc.vector.tensor_tensor(small[:, 2 * a:2 * a + 2, :], small[:, 2 * a:2 * a + 2, :],
                                        sums_b[k][:].rearrange("p (c f) -> p c f", c=2), ALU.max
                                        ).then_inc(sums_free, 1)

            def columns(s, name, n, src, sc):
                use, _ = PROJ.use(s, "proj" + name, n - 1)
                dve.wait_ge(proj_free, use + 1)
                if name == "1":
                    for g in range(2):
                        nc.vector.tensor_copy(sc.cols[:, :, 2 * g:2 * g + 2], src[:, :, g, 256:258])
                        last = nc.vector.tensor_copy(sc.cols[:, :, 32 + 2 * g:34 + 2 * g], src[:, :, g, 258:260])
                else:
                    nc.vector.tensor_copy(sc.cols[:, :, 0:1], src[:, :, DIM:DIM + 1])
                    last = nc.vector.tensor_copy(sc.cols[:, :, 32:33], src[:, :, DIM + 1:DIM + 2])
                last.then_inc(cols_made[int(name) - 1], 1)

            def step(s):
                begun = settled[0] = count_before(s, SETTLED)
                if not s.looped and s.t == 0:
                    prepare_w1()
                    prepare_w2_w3()
                if s.tail:
                    use, k = ROWS.use(s, "shift3")
                    dve.wait_ge(rows_full, use + 1)
                    nc.vector.tensor_scalar(low_col[:], sc3.cols[:, :, 32], rows_b[k][:, 0:1], 0.0,
                                            ALU.subtract, ALU.max).then_inc(rows_free, 1)
                    dve.wait_ge(rows_free, use + 1)
                    nc.vector.tensor_scalar(keep[:], count[s.tail.slot][:], 1.0, None, ALU.min)
                    settle(nc.vector.tensor_scalar(low_col[:], low_col[:], -FALL, None, ALU.mult))
                    settle(nc.vector.tensor_scalar(empty[:], keep[:], -1.0, 1.0, ALU.mult, ALU.add))
                if s.back:
                    head_out(3, [SUMS.last(s, 2), SUMS.last(s, 1)])
                if s.tail:
                    use, k = ROWS.use(s, "q3")
                    dve.wait_ge(low_row_made, s.tail.n + 1)
                    for c in range(NC):
                        nc.vector.scalar_tensor_tensor(out=expo[:, c, :], in0=low_row[:], scalar=low_col[:, c:c + 1],
                                                       in1=rows_b[k][:], op0=ALU.add, op1=ALU.max
                                                       ).then_inc(expo_made, 1)
                    nc.vector.engine_nop().then_inc(rows_free, 1)
                if s.back:
                    elu_out(s, s.back, 3)
                if s.tail:
                    weights3(s, 0)
                    weights3(s, 1)
                if s.front:
                    columns(s, "1", 2 * NC, xl1, sc1)
                if s.tail:
                    weights3(s, 2)
                if s.front:
                    rows_of(s, s.front, "1", 0, sc1)
                if s.tail:
                    weights3(s, 3)
                if s.front:
                    use, _ = TURN.use(s, "mask", 1)
                    dve.wait_ge(turn_full, use + 1)
                    for c in range(NC):
                        own = mask[s.front.slot][:, c, c * P:(c + 1) * P]
                        last = nc.vector.tensor_tensor(own, own, ident_b[:], ALU.max)
                    settle(last)
                    split(s.front, 0, sc1)
                    shifted(s, "1", sc1)
                if s.after:
                    k = s.after.slot
                    dve.wait_ge(x_loaded[k], s.after.half * 16 + 16)
                    half_moments(norm1, x_in[k])
                if s.front:
                    head_weights(s, 0, range(0, 2))
                if s.after:
                    moments(0, norm1)
                if s.back:
                    columns(s, "2", NC, xl2, sc2)
                if s.front:
                    head_weights(s, 0, range(2, 4))
                if s.back:
                    rows_of(s, s.back, "2", 1, sc2)
                    split(s.back, 1, sc2)
                    shifted(s, "2", sc2)
                if s.tail:
                    leaky_sums(s, 0)
                if s.back:
                    weights(s, s.back, "q2", 0, 1, sc2, prob2)
                if s.tail:
                    leaky_sums(s, 1)
                if s.front:
                    head_weights(s, 1, range(0, 2))
                    head_out(0, [SUMS.use(s, "head0", a) for a in range(2)])
                    head_weights(s, 1, range(2, 4))
                if s.back:
                    layer_out(s, 0)
                if s.front:
                    elu_out(s, s.front, 0)
                if s.back:
                    layer_out(s, 1)
                if s.front:
                    head_weights(s, 2, range(0, 2))
                if s.back:
                    layer_out(s, 2)
                if s.front:
                    head_weights(s, 2, range(2, 4))
                if s.back:
                    layer_out(s, 3)
                    use, _ = SUMS.use(s, "sum2", NC - 1)
                    dve.wait_ge(sums_free, use + 1)
                    half_moments(norm2, xb[s.back.slot])
                if s.front:
                    head_out(1, [SUMS.use(s, "head1", a) for a in range(2)])
                if s.back:
                    moments(1, norm2)
                if s.front:
                    head_weights(s, 3, range(0, 2))
                if s.back:
                    normalise(s.back, 1, norm2, xb[s.back.slot])
                if s.front:
                    elu_out(s, s.front, 1)
                    head_weights(s, 3, range(2, 4))
                if s.after:
                    normalise(s.after, 0, norm1, x_in[s.after.slot])
                if s.front:
                    head_out(2, [SUMS.use(s, "head2", a) for a in range(2)])
                if s.after:
                    k = s.after.slot
                    dve.wait_ge(adj_loaded[k], s.after.half * 16 + 16)
                    nc.vector.tensor_scalar(mask[k][:], adj_in[k][:], 0, None, ALU.is_gt).then_inc(mask_made, 1)
                if s.front:
                    elu_out(s, s.front, 2)
                if s.back:
                    columns(s, "3", NC, xl3, sc3)
                    rows_of(s, s.back, "3", 2, sc3)
                    split(s.back, 2, sc3)
                assert s.looped or settled[0] - begun == sum(SETTLED[g] for g in SETTLED if s.has(g))

            steps(dve, step)

        @block.tensor
        def _(pe):
            def turn_bank(s, name, i=0):
                use, b = TURN.use(s, name, i)
                if older(use):
                    pe.wait_ge(turn_free, use - 1)
                return turn_b[b]

            def rows_bank(s, name):
                use, b = ROWS.use(s, name)
                if older(use):
                    pe.wait_ge(rows_free, use - 1)
                return rows_b[b]

            def turn_nodes(s, b, name, which, norm):
                pe.wait_ge(hn_made[which], b.n + 1)
                for k in range(KC):
                    T = turn_bank(s, name, k)
                    for c in range(NC):
                        last = nc.tensor.transpose(T[:, c * P:(c + 1) * P], norm.out[:, c, k * P:(k + 1) * P], ident[:])
                    last.then_inc(turn_full, 1)

            def project(s, name, i, lhs, w):
                use, b = PROJ.use(s, name, i)
                if older(use):
                    pe.wait_ge(proj_free, use - 1)
                n = w[0].shape[-1]
                for k in range(len(lhs)):
                    last = nc.tensor.matmul(proj_b[b][:, 0:n], lhs[k], w[k], start=(k == 0), stop=(k == len(lhs) - 1))
                last.then_inc(proj_full, 1)

            def rows(s, b, name, which, sc):
                pe.wait_ge(cols_made[which], b.n + 1)
                R = rows_bank(s, "rows" + name)
                for c in range(NC):
                    last = nc.tensor.transpose(R[:, c * P:(c + 1) * P], sc.cols[:, c, :], ident[:])
                last.then_inc(rows_full, 1)

            def shift(s, b, name, which, sc):
                pe.wait_ge(diag_made[which], b.n + 1)
                R = rows_bank(s, "shift" + name)
                nc.tensor.matmul(R[:, 0:sc.heads], ones[:], sc.diag[:, 0:sc.heads], start=True, stop=True
                                 ).then_inc(rows_full, 1)

            def spread_row(s, b, name, i, which, sc):
                pe.wait_ge(split_made[which], b.n + 1)
                R = rows_bank(s, name)
                nc.tensor.matmul(R[:], pick[:, i, :], sc.split[:], start=True, stop=True).then_inc(rows_full, 1)

            def weigh(s, name, i, j, per_bank, which, weight, of, n, y, d):
                use, k = SUMS.use(s, name, i)
                if j == 0 and older(use):
                    pe.wait_ge(sums_free, use - 1)
                for c in range(NC):
                    if d == 0:
                        pe.wait_ge(prob_full[which], of + (c + 1))
                    last = nc.tensor.matmul(sums_b[k][:, j * n:(j + 1) * n], weight[:, c, d * P:(d + 1) * P], y(c),
                                            start=(c == 0), stop=(c == NC - 1))
                if j == per_bank - 1:
                    last.then_inc(sums_full, 1)

            def head(s, h, a):
                if a == 0:
                    pe.wait_ge(y1_made, s.front.n * HEADS + (h + 1))
                for j in range(2):
                    weigh(s, f"head{h}", a, j, 2, 0, prob1[h % 2], s.front.n * (HEADS * NC) + h * NC, HEAD_DIM + 1,
                          lambda c: y1[:, c, h, :], 2 * a + j)

            def turn_elu(s, b, h):
                pe.wait_ge(elu_made, b.n * HEADS + (h + 1))
                T = turn_bank(s, f"elu{h}")
                for c in range(NC):
                    last = nc.tensor.transpose(T[:, c * P:(c + 1) * P], elu[h % 2][:, c, :], ident[:])
                last.then_inc(turn_full, 1)

            def proj1(s, c):
                for g in range(2):
                    project(s, "proj1", 2 * c + g, [norm1.T[:, k, c * P:(c + 1) * P] for k in range(KC)],
                            [w1[:, k, g, :] for k in range(KC)])

            def proj2(s, c):
                project(s, "proj2", c, [h2T[:, k, c * P:(c + 1) * P] for k in range(HEADS)],
                        [w2[:, k, :] for k in range(HEADS)])

            def sum2(s, d):
                weigh(s, "sum2", d, 0, 1, 1, prob2, s.back.n * NC, DIM + 1, lambda c: y2[:, c, :], d)

            def sum3(s, d):
                weigh(s, "sum3", d // 2, d % 2, 2, 2, prob3, s.tail.n * NC, DIM, lambda c: y3[:, c, :], d)

            def step(s):
                if s.front:
                    pe.wait_ge(turn_free, TURN.before(s)[0] - (1 if s.looped or s.t > 0 else 0))
                    if not s.looped and s.t == 0:
                        pe.wait_ge(w1_ready, 1)
                if s.tail:
                    shift(s, s.tail, "3", 2, sc3)
                if s.front:
                    proj1(s, 0)
                if s.tail:
                    spread_row(s, s.tail, "q3", 0, 2, sc3)
                if s.front:
                    for c in range(1, NC):
                        proj1(s, c)
                if s.back:
                    turn_elu(s, s.back, 3)
                if s.front:
                    pe.wait_ge(mask_made, s.front.n + 1)
                    for j in range(2):
                        T = turn_bank(s, "mask", j)[:].bitcast(BF16)
                        for k in range(2):
                            for c in range(NC):
                                at = k * NODES + c * P
                                last = nc.tensor.transpose(T[:, at:at + P],
                                                           mask[s.front.slot][:, c, (2 * j + k) * P:(2 * j + k + 1) * P],
                                                           ident_b[:])
                        last.then_inc(turn_full, 1)
                    rows(s, s.front, "1", 0, sc1)
                if s.back:
                    use, _ = TURN.use(s, "elu3")
                    pe.wait_ge(turn_free, use + 1)
                    if not s.looped and s.t == 1:
                        pe.wait_ge(w_ready, 1)
                    proj2(s, 0)
                    proj2(s, 1)
                if s.front:
                    shift(s, s.front, "1", 0, sc1)
                if s.back:
                    proj2(s, 2)
                if s.front:
                    spread_row(s, s.front, "q1_0", 0, 0, sc1)
                if s.back:
                    proj2(s, 3)
                if s.tail:
                    pe.wait_ge(y3_made, s.tail.n * NC + NC)
                    sum3(s, 0)
                if s.back:
                    rows(s, s.back, "2", 1, sc2)
                if s.tail:
                    sum3(s, 1)
                if s.back:
                    shift(s, s.back, "2", 1, sc2)
                if s.tail:
                    sum3(s, 2)
                if s.back:
                    spread_row(s, s.back, "q2", 0, 1, sc2)
                if s.tail:
                    sum3(s, 3)
                if s.front:
                    head(s, 0, 0)
                    spread_row(s, s.front, "q1_1", 1, 0, sc1)
                    head(s, 0, 1)
                if s.back:
                    pe.wait_ge(y2_made, s.back.n * NC + NC)
                    sum2(s, 0)
                if s.front:
                    spread_row(s, s.front, "q1_2", 2, 0, sc1)
                if s.back:
                    for d in range(1, NC):
                        sum2(s, d)
                if s.front:
                    head(s, 1, 0)
                    head(s, 1, 1)
                    spread_row(s, s.front, "q1_3", 3, 0, sc1)
                    turn_elu(s, s.front, 0)
                    head(s, 2, 0)
                    head(s, 2, 1)
                if s.back:
                    turn_nodes(s, s.back, "hn2", 1, norm2)
                if s.front:
                    turn_elu(s, s.front, 1)
                if s.back:
                    use, _ = TURN.use(s, "hn2", KC - 1)
                    pe.wait_ge(turn_free, use + 1)
                    for c in range(NC):
                        project(s, "proj3", c, [norm2.T[:, k, c * P:(c + 1) * P] for k in range(KC)],
                                [w3[:, k, :] for k in range(KC)])
                if s.after:
                    turn_nodes(s, s.after, "hn1", 0, norm1)
                if s.front:
                    head(s, 3, 0)
                if s.back:
                    rows(s, s.back, "3", 2, sc3)
                if s.front:
                    turn_elu(s, s.front, 2)
                    head(s, 3, 1)

            pe.wait_ge(pool_consts, 2)
            steps(pe, step)


_INS = ["x", "adj", "L0_gnn_W1", "L0_gnn_att_src1", "L0_gnn_att_dst1", "L0_gnn_b1", "L0_gnn_W2",
        "L0_gnn_att_src2", "L0_gnn_att_dst2", "L0_gnn_b2", "L1_gnn_W", "L1_gnn_a"]


def kernel(**inputs):
    import numpy as _np
    import concourse.bacc as _bacc
    from concourse import mybir as _mybir
    from concourse.bass_utils import run_bass_kernel_spmd as _run

    nc = _bacc.Bacc("TRN2", target_bir_lowering=False, num_devices=1)
    arrays, args = {}, []
    for name in _INS:
        a = _np.ascontiguousarray(inputs[name])
        arrays[f"in_{name}"] = a
        args.append(nc.dram_tensor(f"in_{name}", a.shape, _mybir.dt.from_np(a.dtype), kind="ExternalInput").ap())
    out = nc.dram_tensor("out_x", (BATCHES, NODES, DIM), F32, kind="ExternalOutput").ap()
    gat_block(nc, *args, out)
    r = _run(nc, [arrays], core_ids=[0])
    return r.results[0]["out_x"]
```

```python
from contextlib import ExitStack
from typing import NamedTuple

import concourse.bass as bass
from concourse import mybir

P = 128
F32 = mybir.dt.float32
F32R = mybir.dt.float32r
BF16 = mybir.dt.bfloat16
I32 = mybir.dt.int32
ALU = mybir.AluOpType
ACT = mybir.ActivationFunctionType
AX = mybir.AxisListType

BATCHES = 16
NODES = 512
DIM = 256
HEADS = 4
HEAD_DIM = 128
WIDE = HEADS * HEAD_DIM
W1_WIDTH = WIDE + 32 + HEADS
NC = NODES // P
KC = DIM // P
EPS = 1e-5
SLOPE = 0.2
FALL = 1.0 - SLOPE


GRAPHS = {"after": -1, "front": 0, "back": 1, "tail": 2}
SETTLED = {"after": 1, "front": 10, "back": 7, "tail": 2}


class Graph(NamedTuple):
    n: object
    half: object
    slot: int


class Step:

    def __init__(self, t, even=None):
        self.t = t if even is None else even * 2 + (2 + t)
        self.looped = even is not None
        self.parity = t % 2

        def graph(back):
            if even is None:
                n = t - back
                return Graph(n, n // 2, n % 2) if 0 <= n < BATCHES else None
            m = 2 + t - back
            return Graph(even * 2 + m, even + m // 2, m % 2)

        self.after, self.front, self.back, self.tail = graph(-1), graph(0), graph(1), graph(2)

    def has(self, graph):
        graphs = {"after": self.after, "front": self.front, "back": self.back, "tail": self.tail}
        return graphs[graph] is not None


def count_before(s, of):
    if s.looped:
        return s.t * sum(of.values()) + (of["after"] - of["back"] - 2 * of["tail"])
    return sum(of[g] * min(max(s.t - late, 0), BATCHES) for g, late in GRAPHS.items())


GROUP1 = (slice(0, WIDE // 2), slice(WIDE // 2, W1_WIDTH))


class Ring:

    def __init__(self, *order):
        self.order = order
        self.of = {g: sum(c for _, graph, c in order if graph == g) for g in GRAPHS}
        assert sum(self.of.values()) % 2 == 0

    def before(self, s):
        n = count_before(s, self.of)
        return n, (self.of["after"] + self.of["back"]) % 2 if s.looped else n % 2

    def use(self, s, name, i=0):
        at = i
        for what, graph, count in self.order:
            if what == name:
                break
            if s.has(graph):
                at += count
        base, odd = self.before(s)
        return base + at, (odd + at) % 2

    def last(self, s):
        base, odd = self.before(s)
        return base - 1, (odd + 1) % 2


def older(use):
    return not isinstance(use, int) or use >= 2


TURN = Ring(("mask", "front", 2), ("hn1", "after", KC), ("elu0", "front", 1), ("hn2", "back", KC),
            ("elu1", "front", 1), ("elu2", "front", 1), ("elu3", "front", 1))
PROJ = Ring(("proj1", "front", 2 * NC), ("proj2", "back", NC), ("proj3", "back", NC))
SUMS = Ring(("sum3", "tail", 2), ("head0", "front", 2), ("sum2", "back", NC), ("head1", "front", 2),
            ("head2", "front", 2), ("head3", "front", 2))
WHOLE = Ring(("hn1", "after", KC), ("elu0", "front", 1), ("hn2", "back", KC), ("elu1", "front", 1),
             ("elu2", "front", 1), ("elu3", "front", 1))
ROWS = Ring(("shift3", "tail", 1), ("q3", "tail", 1), ("rows1", "front", 1), ("shift1", "front", 1),
            ("q1_0", "front", 1), ("rows2", "back", 1), ("shift2", "back", 1), ("q2", "back", 1),
            ("q1_1", "front", 1), ("q1_2", "front", 1), ("q1_3", "front", 1), ("rows3", "back", 1))


def steps(engine, step):
    for t in range(-1, 2):
        step(Step(t))
    with engine.Fori(0, (BATCHES - 4) // 2) as i:
        for t in range(2):
            step(Step(t, i))
    for t in range(BATCHES - 2, BATCHES + 2):
        step(Step(t))


def gat_block(nc, x, adj, W1, src1, dst1, b1, W2, src2, dst2, b2, W3, a3, out):
    with ExitStack() as ctx:
        def sb(name, shape, dt=F32):
            return ctx.enter_context(nc.sbuf_tensor(name, shape, dt))

        def bank(name):
            return ctx.enter_context(nc.psum_tensor(name, [P, 512], F32))

        def sem(name):
            return ctx.enter_context(nc.semaphore(name))

        ident = sb("ident", [P, P])
        ident_b = sb("ident_b", [P, P], BF16)
        ones = sb("ones", [P, P])
        pick = sb("pick", [P, HEADS, P], F32R)
        w1 = [sb(f"w1_{i}", [P, KC, W1_WIDTH], F32R) for i in range(2)]
        w2 = [sb(f"w2_{i}", [P, HEADS, DIM + 2], F32R) for i in range(2)]
        w3 = [sb(f"w3_{i}", [P, KC, DIM + 2], F32R) for i in range(2)]
        bias1 = sb("bias1", [P, WIDE])
        bias2 = sb("bias2", [P, DIM])
        minus_one = sb("minus_one", [P, 1])
        eps = sb("eps", [P, NC])
        minus_ones = sb("minus_ones", [P, NC])
        half_power = sb("half_power", [P, NC])

        x_in = [sb(f"x_in{s}", [P, NC, DIM]) for s in range(2)]
        adj_in = sb("adj_in", [P, NC, NODES], I32)
        xb = [sb(f"xb{s}", [P, NC, DIM]) for s in range(2)]
        mask = [sb(f"mask{s}", [P, NC, NODES], BF16) for s in range(2)]
        maskT = [sb(f"maskT{s}", [P, NC, NODES], BF16) for s in range(2)]
        count = [sb(f"count{s}", [P, NC]) for s in range(2)]
        keep = sb("keep", [P, NC])
        empty = sb("empty", [P, NC])

        class Norm:
            def __init__(self, name):
                self.halves = sb(f"halves_{name}", [P, NC, 6])
                self.stats = sb(f"stats_{name}", [P, NC, 2])
                self.var = sb(f"var_{name}", [P, NC])
                self.rstd = sb(f"rstd_{name}", [P, NC])
                self.scaled_mean = sb(f"scaled_mean_{name}", [P, NC])
                self.shift = sb(f"shift_{name}", [P, NC])
                self.out = sb(f"hn_{name}", [P, NC, DIM])
                self.T = [sb(f"hT_{name}_{i}", [P, KC, NODES], F32R) for i in range(2)]

        norm1, norm2 = Norm("1"), Norm("2")

        class Scores:
            def __init__(self, name, heads):
                self.heads = heads
                self.cols = sb(f"cols_{name}", [P, NC, P]) if heads == 1 else xl1[:, :, WIDE:W1_WIDTH]
                self.neg = sb(f"neg_{name}", [P, 1])
                self.diag = sb(f"diag_{name}", [P, HEADS])
                self.split_at = 0 if name == "3" else 32
                self.split = sb(f"split_{name}", [P, NODES], F32R)
                self.rel = sb(f"rel_{name}", [P, NC, heads])
                self.r = sb(f"r_{name}", [P, NC, heads])

            def turned(self, c):
                if self.heads == 1:
                    return self.cols[:, c, :]
                return xl1_flat[:, c * W1_WIDTH + WIDE:c * W1_WIDTH + WIDE + P]

        row = sb("row", [P, NODES])
        relu_row = sb("relu_row", [P, NODES])

        xl1_flat = sb("xl1", [P, NC * W1_WIDTH + P - 32 - HEADS])
        xl1 = xl1_flat[:, 0:NC * W1_WIDTH].rearrange("p (c f) -> p c f", c=NC)
        sc1, sc2, sc3 = Scores("1", HEADS), Scores("2", 1), Scores("3", 1)
        y1 = sb("y1", [P, NC, HEADS, HEAD_DIM + 1])
        xl2 = sb("xl2", [P, NC, DIM + 2])
        xl3 = sb("xl3", [P, NC, DIM + 2])
        prob1 = [sb(f"prob1_{s}", [P, NC, NODES]) for s in range(2)]
        prob2 = sb("prob2", [P, NC, NODES])
        prob3 = sb("prob3", [P, NC, NODES])
        rz1 = sb("rz1", [P, 2 * HEADS, 2])
        z1 = [sb(f"z1_{s}", [P, NC, HEAD_DIM]) for s in range(2)]
        ez = [sb(f"ez_{s}", [P, NC, HEAD_DIM]) for s in range(2)]
        elu = [sb(f"elu_{s}", [P, NC, HEAD_DIM]) for s in range(2)]
        h2T = [sb(f"h2T_{i}", [P, HEADS, NODES], F32R) for i in range(2)]
        whole = [sb(f"whole{i}", [P, NODES]) for i in range(2)]
        rz2 = sb("rz2", [P, NC])
        low_row = sb("low_row", [P, NODES])
        low_col = sb("low_col", [P, NC])
        z3 = sb("z3", [P, NC])
        rz3 = sb("rz3", [P, NC])
        small = sb("small", [P, NC, DIM])
        o = sb("o", [P, NC, DIM])
        w1_whole = prob2[:].rearrange("p c n -> p (c n)")[:, 0:KC * W1_WIDTH
                                                          ].rearrange("p (k f) -> p k f", k=KC)
        w23_whole = prob1[1][:].rearrange("p c n -> p (c n)")[:, 0:(HEADS + KC) * (DIM + 2)
                                                              ].rearrange("p (k f) -> p k f", k=HEADS + KC)
        w2_whole, w3_whole = w23_whole[:, 0:HEADS, :], w23_whole[:, HEADS:HEADS + KC, :]
        att1 = o[:].rearrange("p c f -> p (c f)").rearrange("p (t n) -> p t n", t=2)
        att2, att3 = small[:, 0:2, :], small[:, 2:4, :]
        pick_f = low_row[:].rearrange("p (h m) -> p h m", h=HEADS)

        turn_b = [bank(f"turn{i}") for i in range(2)]
        proj_b = [bank(f"proj{i}") for i in range(2)]
        sums_b = [bank(f"sums{i}") for i in range(2)]
        rows_b = [bank(f"rows{i}") for i in range(2)]

        w1_loaded = sem("w1_loaded")
        w_loaded = sem("w_loaded")
        x_loaded = [sem(f"x_loaded{s}") for s in range(2)]
        adj_loaded = sem("adj_loaded")
        out_stored = sem("out_stored")
        pool_consts = sem("pool_consts")
        w1_ready = sem("w1_ready")
        w_ready = sem("w_ready")
        w_settled = sem("w_settled")
        w_hi_made = sem("w_hi_made")
        features_split = sem("features_split")
        dve_settled = sem("dve_settled")
        pool_settled = sem("pool_settled")
        eps_added = [sem(f"eps_added{i}") for i in range(2)]
        mask_made = sem("mask_made")
        xb_made = sem("xb_made")
        var_made = [sem(f"var_made{i}") for i in range(2)]
        rstd_made = [sem(f"rstd_made{i}") for i in range(2)]
        mean_scaled = [sem(f"mean_scaled{i}") for i in range(2)]
        shift_made = [sem(f"shift_made{i}") for i in range(2)]
        hn_made = [sem(f"hn_made{i}") for i in range(2)]
        turn_full, turn_free = sem("turn_full"), sem("turn_free")
        hi_made, lo_made = sem("hi_made"), sem("lo_made")
        proj_full, proj_free = sem("proj_full"), sem("proj_free")
        sums_full, sums_free = sem("sums_full"), sem("sums_free")
        rows_full, rows_free = sem("rows_full"), sem("rows_free")
        prob_full = [sem(f"prob_full{i}") for i in range(3)]
        cols_made = {i: sem(f"cols_made{i}") for i in (1, 2)}
        diag_made = [sem(f"diag_made{i}") for i in range(3)]
        row_made = [sem(f"row_made{i}") for i in range(2)]
        split_made = [sem(f"split_made{i}") for i in range(3)]
        r_made = [sem(f"r_made{i}") for i in range(2)]
        y1_made = sem("y1_made")
        y2_made = sem("y2_made")
        y3_made = sem("y3_made")
        ez_made = sem("ez_made")
        elu_made = sem("elu_made")
        low_row_made = sem("low_row_made")
        expo_made = sem("expo_made")
        e3_made = sem("e3_made")
        rz3_made = sem("rz3_made")
        small_made = sem("small_made")
        out_made = sem("out_made")

        x_v = x.rearrange("b (c p) d -> b p c d", p=P)
        adj_v = adj.rearrange("b (c p) d -> b p c d", p=P)
        out_v = out.rearrange("b (c p) d -> b p c d", p=P)

        def spread(row):
            return row.to_broadcast([P, row.shape[1]])

        block = ctx.enter_context(nc.Block())

        @block.sync
        def _(sp):
            sp.dma_start(x_in[0][:], x_v[0]).then_inc(x_loaded[0], 16)
            sp.dma_start(w1_whole[:, :, 0:WIDE], W1.rearrange("(c p) n -> p c n", p=P)).then_inc(w1_loaded, 16)
            sp.dma_start(att1[:, 0, :], spread(src1.rearrange("(o h) f -> o (h f)", o=1))).then_inc(w1_loaded, 16)
            sp.dma_start(att1[:, 1, :], spread(dst1.rearrange("(o h) f -> o (h f)", o=1))).then_inc(w1_loaded, 16)
            sp.dma_start(adj_in[:], adj_v[0]).then_inc(adj_loaded, 16)
            sp.dma_start(w2_whole[:, :, 0:DIM], W2.rearrange("(c p) n -> p c n", p=P)).then_inc(w_loaded, 16)
            sp.dma_start(att2[:, 0, :], spread(src2)).then_inc(w_loaded, 16)
            sp.dma_start(att2[:, 1, :], spread(dst2)).then_inc(w_loaded, 16)
            sp.dma_start(w3_whole[:, :, 0:DIM], W3.rearrange("(c p) n -> p c n", p=P)).then_inc(w_loaded, 16)
            a3_v = a3.rearrange("(t f) o -> t (f o)", t=2)
            sp.dma_start(att3[:, 0, :], spread(a3_v[0:1, :])).then_inc(w_loaded, 16)
            sp.dma_start(att3[:, 1, :], spread(a3_v[1:2, :])).then_inc(w_loaded, 16)
            sp.dma_start(bias1[:], spread(b1.rearrange("(o n) -> o n", o=1))).then_inc(w_loaded, 16)
            sp.dma_start(bias2[:], spread(b2.rearrange("(o n) -> o n", o=1))).then_inc(w_loaded, 16)
            sp.dma_start(x_in[1][:], x_v[1]).then_inc(x_loaded[1], 16)

            def step(s):
                if s.front and s.after:
                    sp.wait_ge(mask_made, s.front.n + 1)
                    sp.dma_start(adj_in[:], adj_v[s.after.n]).then_inc(adj_loaded, 16)
                if s.tail:
                    sp.wait_ge(out_made, s.tail.n * 2 + 2)
                    sp.dma_start(out_v[s.tail.n], o[:]).then_inc(out_stored, 16)
                if s.front and (s.looped or s.t < BATCHES - 2):
                    sp.wait_ge(xb_made, s.front.n + 1)
                    sp.wait_ge(hn_made[0], s.front.n + 1)
                    sp.dma_start(x_in[s.front.slot][:], x_v[s.front.n + 2]).then_inc(x_loaded[s.front.slot], 16)

            steps(sp, step)
            sp.wait_ge(out_stored, 16 * BATCHES)

        @block.gpsimd
        def _(pool):
            nc.gpsimd.memset(half_power[:], -0.5)
            nc.gpsimd.memset(eps[:], EPS)
            nc.gpsimd.memset(minus_ones[:], -1.0)
            nc.gpsimd.memset(ident[:], 0.0).then_inc(pool_settled, 1)
            nc.gpsimd.memset(pick_f, 0.0).then_inc(pool_settled, 1)
            pool.wait_ge(pool_settled, 2)
            nc.gpsimd.affine_select(out=ident[:], in_=ident[:], compare_op=ALU.not_equal, fill=1.0, base=0,
                                    pattern=[[-1, P]], channel_multiplier=1).then_inc(pool_consts, 1)
            for lift in (0, 32):
                nc.gpsimd.affine_select(out=pick_f, in_=pick_f, compare_op=ALU.not_equal, fill=1.0, base=-lift,
                                        pattern=[[-1, HEADS], [0, P]], channel_multiplier=1).then_inc(pool_settled, 1)
                pool.wait_ge(pool_settled, 3 + lift // 32)
            nc.gpsimd.tensor_copy(pick[:], pick_f).then_inc(pool_consts, 1)

            def rstd(b, which, norm):
                pool.wait_ge(var_made[which], b.n + 1)
                nc.gpsimd.tensor_tensor(norm.var[:], norm.stats[:, :, 1], eps[:], ALU.add
                                        ).then_inc(eps_added[which], 1)
                pool.wait_ge(eps_added[which], b.n + 1)
                nc.gpsimd.tensor_tensor(norm.rstd[:], norm.var[:], half_power[:], ALU.pow
                                        ).then_inc(rstd_made[which], 1)
                pool.wait_ge(rstd_made[which], b.n + 1)
                nc.gpsimd.tensor_tensor(norm.scaled_mean[:], norm.stats[:, :, 0], norm.rstd[:], ALU.mult
                                        ).then_inc(mean_scaled[which], 1)
                pool.wait_ge(mean_scaled[which], b.n + 1)
                nc.gpsimd.tensor_tensor(norm.shift[:], norm.scaled_mean[:], minus_ones[:], ALU.mult
                                        ).then_inc(shift_made[which], 1)

            def split_w1():
                pool.wait_ge(w_hi_made, 1)
                nc.gpsimd.tensor_tensor(w1[1][:, :, 0:WIDE], w1_whole[:, :, 0:WIDE],
                                        w1[0][:, :, 0:WIDE].bitcast(F32), ALU.subtract).then_inc(features_split, 1)

            def split_w2_w3():
                pool.wait_ge(w_hi_made, 2)
                for w, w_whole in ((w2, w2_whole), (w3, w3_whole)):
                    nc.gpsimd.tensor_tensor(w[1][:, :, 0:DIM], w_whole[:, :, 0:DIM], w[0][:, :, 0:DIM].bitcast(F32),
                                            ALU.subtract).then_inc(features_split, 1)

            def lesser(s, name, i, parts, at):
                use, b = WHOLE.use(s, name, i)
                pool.wait_ge(hi_made, use + 1)
                nc.gpsimd.tensor_tensor(parts[1][:, at, :], whole[b][:], parts[0][:, at, :].bitcast(F32), ALU.subtract
                                        ).then_inc(lo_made, 1)

            def step(s):
                if not s.looped and s.t == 0:
                    split_w2_w3()
                if s.front:
                    pool.wait_ge(r_made[0], s.front.n + 1)
                    for h in range(HEADS):
                        nc.gpsimd.tensor_tensor(
                            y1[:, :, h, 0:HEAD_DIM], xl1[:, :, h * HEAD_DIM:(h + 1) * HEAD_DIM],
                            y1[:, :, h, HEAD_DIM:HEAD_DIM + 1].to_broadcast([P, NC, HEAD_DIM]), ALU.mult
                        ).then_inc(y1_made, 1)
                if s.after:
                    rstd(s.after, 0, norm1)
                if not s.looped and s.t == -1:
                    split_w1()
                if s.tail:
                    if s.looped or s.tail.n > 0:
                        pool.wait_ge(out_stored, s.tail.n * 16)
                    for a in range(2):
                        use, _ = SUMS.use(s, "sum3", a)
                        pool.wait_ge(sums_free, use + 1)
                        at = slice(2 * a, 2 * a + 2)
                        nc.gpsimd.tensor_tensor(o[:, at, :], small[:, at, :], xb[s.tail.slot][:, at, :], ALU.add
                                                ).then_inc(out_made, 1)
                if s.front:
                    if s.tail:
                        pool.wait_ge(out_made, s.tail.n * 2 + 2)
                    if not s.looped and s.t == 0:
                        pool.wait_ge(w_loaded, 16 * 8)
                    pool.wait_ge(x_loaded[s.front.slot], s.front.half * 16 + 16)
                    nc.gpsimd.tensor_tensor(xb[s.front.slot][:], x_in[s.front.slot][:],
                                            bias2[:, None, :].to_broadcast([P, NC, DIM]), ALU.add
                                            ).then_inc(xb_made, 1)
                if s.after:
                    for c in range(KC):
                        lesser(s, "hn1", c, norm1.T, c)
                if s.back:
                    rstd(s.back, 1, norm2)
                if s.front:
                    lesser(s, "elu0", 0, h2T, 0)
                if s.back:
                    for c in range(KC):
                        lesser(s, "hn2", c, norm2.T, c)
                if s.front:
                    lesser(s, "elu1", 0, h2T, 1)
                    lesser(s, "elu2", 0, h2T, 2)
                    lesser(s, "elu3", 0, h2T, 3)

            steps(pool, step)

        @block.scalar
        def _(act):
            def from_proj(s, name, i, dst):
                use, b = PROJ.use(s, name, i)
                act.wait_ge(proj_full, use + 1)
                nc.scalar.copy(dst, proj_b[b][:, 0:dst.shape[-1]]).then_inc(proj_free, 1)

            def turned_whole(s, name, i, function, bias):
                use, b = TURN.use(s, name, i)
                act.wait_ge(turn_full, use + 1)
                use, k = WHOLE.use(s, name, i)
                if older(use):
                    act.wait_ge(lo_made, use - 1)
                nc.scalar.activation(whole[k][:], turn_b[b][:], function, bias=bias).then_inc(turn_free, 1)

            def turned_hi(s, name, i, parts, at):
                use, _ = TURN.use(s, name, i)
                act.wait_ge(turn_free, use + 1)
                nc.scalar.copy(parts[0][:, at, :], whole[WHOLE.use(s, name, i)[1]][:]).then_inc(hi_made, 1)

            def relu_of_row(s, b, name, which, sc):
                use, k = ROWS.use(s, "rows" + name)
                act.wait_ge(diag_made[which], b.n + 1)
                at = slice(sc.split_at, sc.split_at + sc.heads)
                nc.scalar.activation(relu_row[at, :], rows_b[k][at, :], ACT.Relu, bias=sc.neg[at, :]).then_inc(rows_free, 1)

            def q_row(s, b, name, which, sc):
                use, _ = ROWS.use(s, "rows" + name)
                at = slice(sc.split_at, sc.split_at + sc.heads)
                act.wait_ge(rows_free, use + 1)
                nc.scalar.activation(sc.split[at, :], relu_row[at, :], ACT.Exp, scale=-FALL)
                nc.scalar.activation(row[at, :], relu_row[at, :], ACT.Exp, scale=-FALL).then_inc(row_made[which], 1)

            def row3(s, part):
                use, k = ROWS.last(s)
                if part == 0:
                    act.wait_ge(diag_made[2], s.tail.n + 1)
                    nc.scalar.activation(sc3.split[0:1, :], rows_b[k][0:1, :], ACT.Identity, bias=sc3.neg[0:1, :])
                else:
                    nc.scalar.activation(row[0:1, :], rows_b[k][0:1, :], ACT.Identity, bias=sc3.neg[0:1, :]
                                         ).then_inc(rows_free, 1)

            def normalise(b, which, norm, src, chunks):
                act.wait_ge(shift_made[which], b.n + 1)
                for c in chunks:
                    last = nc.scalar.activation(norm.out[:, c, :], src[:, c, :], ACT.Identity,
                                                scale=norm.rstd[:, c:c + 1], bias=norm.shift[:, c:c + 1])
                last.then_inc(hn_made[which], 1)

            def r_cols(s, name, which, sc, low):
                use, _ = ROWS.use(s, "shift" + name)
                act.wait_ge(rows_free, use + 1)
                nc.scalar.activation(sc.r[:], sc.rel[:], ACT.Exp, scale=FALL)
                nc.scalar.activation(low, sc.rel[:], ACT.Exp, scale=SLOPE).then_inc(r_made[which], 1)

            def elu_exp(h, use):
                act.wait_ge(sums_free, use + 1)
                nc.scalar.activation(ez[h % 2][:], z1[h % 2][:], ACT.Exp, bias=minus_one[:]).then_inc(ez_made, 1)

            def elu_turned(s, h):
                turned_whole(s, f"elu{h}", 0, ACT.Identity, minus_one[:])
                turned_hi(s, f"elu{h}", 0, h2T, h)

            def low_sums(s, a):
                use, b = SUMS.use(s, "sum3", a)
                act.wait_ge(sums_full, use + 1)
                nc.scalar.activation(small[:, 2 * a:2 * a + 2, :], sums_b[b][:].rearrange("p (c f) -> p c f", c=2),
                                     ACT.Copy, scale=SLOPE).then_inc(small_made, 1)

            def mask_turned(s, j):
                use, b = TURN.use(s, "mask", j)
                act.wait_ge(turn_full, use + 1)
                for k in range(2):
                    c = 2 * j + k
                    last = nc.scalar.activation(maskT[s.front.slot][:, c, :],
                                                turn_b[b][:].bitcast(BF16)[:, k * NODES:(k + 1) * NODES], ACT.Copy,
                                                accum_out=count[s.front.slot][:, c:c + 1])
                last.then_inc(turn_free, 1)

            def exps3(s, c):
                act.wait_ge(expo_made, s.tail.n * NC + (c + 1))
                nc.scalar.activation(prob3[:, c, :], prob3[:, c, :], ACT.Exp, scale=keep[:, c:c + 1]).then_inc(e3_made, 1)

            def scale3(s, c):
                act.wait_ge(rz3_made, s.tail.n * NC + (c + 1))
                nc.scalar.activation(xl3[:, c, 0:DIM], xl3[:, c, 0:DIM], ACT.Copy, scale=rz3[:, c:c + 1]).then_inc(y3_made, 1)

            def proj1(s, c):
                for g in range(2):
                    from_proj(s, "proj1", 2 * c + g, xl1[:, c, GROUP1[g]])

            def round_w1():
                act.wait_ge(w1_loaded, 16 * 3)
                nc.scalar.copy(w1[0][:, :, 0:WIDE], w1_whole[:, :, 0:WIDE]).then_inc(w_hi_made, 1)

            def round_w2_w3():
                act.wait_ge(w_loaded, 16 * 8)
                nc.scalar.copy(w2[0][:, :, 0:DIM], w2_whole[:, :, 0:DIM])
                nc.scalar.copy(w3[0][:, :, 0:DIM], w3_whole[:, :, 0:DIM]).then_inc(w_hi_made, 1)

            def step(s):
                if not s.looped and s.t == -1:
                    round_w1()
                if not s.looped and s.t == 0:
                    round_w2_w3()
                if s.front:
                    if s.looped or s.t != 0:
                        act.wait_ge(y1_made, s.front.n * HEADS)
                    from_proj(s, "proj1", 0, xl1[:, 0, GROUP1[0]])
                if s.tail:
                    row3(s, 0)
                if s.front:
                    from_proj(s, "proj1", 1, xl1[:, 0, GROUP1[1]])
                if s.tail:
                    row3(s, 1)
                if s.front:
                    proj1(s, 1)
                if s.tail:
                    use, b = ROWS.use(s, "q3")
                    act.wait_ge(rows_full, use + 1)
                    nc.scalar.activation(low_row[:], rows_b[b][:], ACT.Copy, scale=SLOPE).then_inc(low_row_made, 1)
                if s.front:
                    proj1(s, 2)
                if s.tail:
                    exps3(s, 0)
                if s.front:
                    proj1(s, 3)
                if s.tail:
                    exps3(s, 1)
                    exps3(s, 2)
                if s.front:
                    relu_of_row(s, s.front, "1", 0, sc1)
                if s.back:
                    from_proj(s, "proj2", 0, xl2[:, 0, :])
                if s.front:
                    q_row(s, s.front, "1", 0, sc1)
                if s.tail:
                    exps3(s, 3)
                    scale3(s, 0)
                if s.back:
                    from_proj(s, "proj2", 1, xl2[:, 1, :])
                if s.tail:
                    scale3(s, 1)
                    scale3(s, 2)
                if s.back:
                    from_proj(s, "proj2", 2, xl2[:, 2, :])
                if s.tail:
                    scale3(s, 3)
                if s.front:
                    r_cols(s, "1", 0, sc1, y1[:, :, :, HEAD_DIM])
                if s.back:
                    from_proj(s, "proj2", 3, xl2[:, 3, :])
                if s.front:
                    mask_turned(s, 0)
                    mask_turned(s, 1)
                if s.tail:
                    low_sums(s, 0)
                if s.back:
                    relu_of_row(s, s.back, "2", 1, sc2)
                    q_row(s, s.back, "2", 1, sc2)
                if s.tail:
                    low_sums(s, 1)
                if s.back:
                    r_cols(s, "2", 1, sc2, xl2[:, :, DIM:DIM + 1])
                    act.wait_ge(r_made[1], s.back.n + 1)
                    for c in range(NC):
                        nc.scalar.activation(xl2[:, c, 0:DIM], xl2[:, c, 0:DIM], ACT.Copy,
                                             scale=xl2[:, c, DIM:DIM + 1]).then_inc(y2_made, 1)
                if s.front:
                    elu_exp(0, SUMS.use(s, "head0", 1)[0])
                if s.after:
                    normalise(s.after, 0, norm1, x_in[s.after.slot], range(NC))
                    for k in range(KC):
                        turned_whole(s, "hn1", k, ACT.Relu, 0.0)
                        turned_hi(s, "hn1", k, norm1.T, k)
                if s.front:
                    elu_turned(s, 0)
                    elu_exp(1, SUMS.use(s, "head1", 1)[0])
                if s.back:
                    normalise(s.back, 1, norm2, xb[s.back.slot], range(NC // 2, NC))
                    for k in range(KC):
                        turned_whole(s, "hn2", k, ACT.Relu, 0.0)
                        turned_hi(s, "hn2", k, norm2.T, k)
                if s.front:
                    elu_exp(2, SUMS.use(s, "head2", 1)[0])
                    elu_turned(s, 1)
                    turned_whole(s, "elu2", 0, ACT.Identity, minus_one[:])
                if s.back:
                    from_proj(s, "proj3", 0, xl3[:, 0, :])
                if s.front:
                    elu_exp(3, SUMS.use(s, "head3", 1)[0])
                if s.back:
                    from_proj(s, "proj3", 1, xl3[:, 1, :])
                if s.front:
                    turned_hi(s, "elu2", 0, h2T, 2)
                if s.back:
                    for c in range(2, NC):
                        from_proj(s, "proj3", c, xl3[:, c, :])
                if s.front:
                    elu_turned(s, 3)

            act.wait_ge(pool_consts, 1)
            nc.scalar.activation(rz2[:], eps[:], ACT.Exp)
            steps(act, step)

        @block.vector
        def _(dve):
            settled = [0]

            def settle(instruction):
                settled[0] = settled[0] + 1
                instruction.then_inc(dve_settled, 1)
                dve.wait_ge(dve_settled, settled[0])

            nc.vector.memset(minus_one[:], -1.0)
            nc.vector.memset(ones[:], 1.0)
            for w in w1:
                nc.vector.memset(w[:, :, WIDE:].bitcast(F32), 0.0)
            nc.vector.memset(xl1_flat[:, NC * W1_WIDTH:], 0.0)
            for sc in (sc2, sc3):
                nc.vector.memset(sc.cols[:], 0.0)
            for sc in (sc1, sc2, sc3):
                nc.vector.memset(sc.diag[:], 0.0)
                nc.vector.memset(sc.split[:].bitcast(F32), 0.0)
            dve.wait_ge(pool_consts, 1)
            nc.vector.tensor_copy(ident_b[:], ident[:])
            prepared = [0]

            def weights_settle(instruction):
                prepared[0] += 1
                instruction.then_inc(w_settled, 1)
                dve.wait_ge(w_settled, prepared[0])

            def split_columns(parts, w_whole):
                weights_settle(nc.vector.tensor_copy(parts[0], w_whole))
                return nc.vector.tensor_tensor(parts[1], w_whole, parts[0].bitcast(F32), ALU.subtract)

            def prepare_w1():
                dve.wait_ge(w1_loaded, 16 * 3)
                for t in range(2):
                    part = prob3[:, 0:KC, :]
                    weights_settle(nc.vector.tensor_tensor(
                        part, w1_whole[:, :, 0:WIDE], att1[:, t, None, :].to_broadcast([P, KC, WIDE]), ALU.mult))
                    weights_settle(nc.vector.tensor_reduce(w1_whole[:, :, WIDE + 32 * t:WIDE + 32 * t + HEADS],
                                                           part.rearrange("p c (h f) -> p c h f", h=HEADS), AX.X, ALU.add))
                    at = slice(WIDE + 32 * t, WIDE + 32 * t + HEADS)
                    last = split_columns([w[:, :, at] for w in w1], w1_whole[:, :, at])
                last.then_inc(w1_ready, 1)

            def prepare_w2_w3():
                dve.wait_ge(w_loaded, 16 * 8)
                for w, w_whole, att, n in ((w2, w2_whole, att2, HEADS), (w3, w3_whole, att3, KC)):
                    for t in range(2):
                        part = prob3[:, 0:n, 0:DIM]
                        weights_settle(nc.vector.tensor_tensor(part, w_whole[:, :, 0:DIM],
                                                               att[:, t, None, :].to_broadcast([P, n, DIM]), ALU.mult))
                        weights_settle(nc.vector.tensor_reduce(w_whole[:, :, DIM + t:DIM + t + 1], part, AX.X, ALU.add))
                    split_columns([half[:, :, DIM:DIM + 2] for half in w], w_whole[:, :, DIM:DIM + 2])
                nc.vector.tensor_scalar(bias1[:], bias1[:], 1.0, None, ALU.add).then_inc(w_ready, 1)

            def half_moments(norm, src, chunks=range(NC)):
                for c in chunks:
                    last = nc.vector.bn_stats(norm.halves[:, c, :], src[:, c, :])
                if chunks[-1] == NC - 1:
                    settle(last)

            def half_moments_x1(s, c):
                use, _ = SUMS.use(s, "sum2", c)
                dve.wait_ge(sums_free, use + 1)
                half_moments(norm2, xb[s.back.slot], range(c, c + 1))

            def moments(which, norm):
                for c in range(NC):
                    last = nc.vector.bn_aggr(norm.stats[:, c, :], norm.halves[:, c, :])
                last.then_inc(var_made[which], 1)

            def rows_of(s, b, name, which, sc):
                use, k = ROWS.use(s, "rows" + name)
                dve.wait_ge(rows_full, use + 1)
                h = sc.heads
                settle(nc.vector.tensor_reduce(sc.neg[0:h, :], rows_b[k][0:h, :], AX.X, ALU.max, negate=True))
                if which < 2:
                    nc.vector.tensor_scalar(sc.neg[32:32 + h, :], sc.neg[0:h, :], -1.0, None, ALU.mult)
                nc.vector.tensor_scalar(sc.diag[0:h, 0:h], ident[0:h, 0:h], sc.neg[0:h, :], None, ALU.mult
                                        ).then_inc(diag_made[which], 1)

            def split(s, b, which, sc):
                if which < 2:
                    dve.wait_ge(row_made[which], b.n + 1)
                else:
                    use, _ = ROWS.last(s)
                    dve.wait_ge(rows_free, use + 1)
                h, hi, lo = sc.heads, sc.split_at, 32 - sc.split_at
                nc.vector.tensor_tensor(sc.split[lo:lo + h, :], row[hi:hi + h, :], sc.split[hi:hi + h, :].bitcast(F32),
                                        ALU.subtract).then_inc(split_made[which], 1)

            def shifted(s, name, sc):
                use, k = ROWS.use(s, "shift" + name)
                dve.wait_ge(rows_full, use + 1)
                h = sc.heads
                nc.vector.tensor_tensor(sc.rel[:], sc.cols[:, :, 0:h],
                                        rows_b[k][:, None, 0:h].to_broadcast([P, NC, h]), ALU.add
                                        ).then_inc(rows_free, 1)

            def weights(s, b, name, i, which, sc, into, chunks=range(NC)):
                use, k = ROWS.use(s, name)
                if chunks[0] == 0:
                    dve.wait_ge(rows_full, use + 1)
                    dve.wait_ge(r_made[which], b.n + 1)
                for c in chunks:
                    nc.vector.scalar_tensor_tensor(out=into[:, c, :], in0=rows_b[k][:], scalar=sc.r[:, c, i:i + 1],
                                                   in1=mask[b.slot][:, c, :], op0=ALU.max, op1=ALU.mult
                                                   ).then_inc(prob_full[which], 1)
                if chunks[-1] == NC - 1:
                    nc.vector.engine_nop().then_inc(rows_free, 1)

            def head_weights(s, h, chunks=range(NC)):
                weights(s, s.front, f"q1_{h}", h, 0, sc1, prob1[h % 2], chunks)

            def head_out(h, a, uses):
                use, k = uses
                dve.wait_ge(sums_full, use + 1)
                S = sums_b[k][:, 0:258].rearrange("p (c f) -> p c f", c=2)
                settle(nc.vector.reciprocal(rz1[:, 2 * h + a, :], S[:, :, HEAD_DIM]))
                for c in range(2):
                    last = nc.vector.scalar_tensor_tensor(
                        out=z1[h % 2][:, 2 * a + c, :], in0=S[:, c, 0:HEAD_DIM], scalar=rz1[:, 2 * h + a, c:c + 1],
                        in1=bias1[:, h * HEAD_DIM:(h + 1) * HEAD_DIM], op0=ALU.mult, op1=ALU.add)
                last.then_inc(sums_free, 1)

            def elu_out(s, b, h):
                dve.wait_ge(ez_made, b.n * HEADS + (h + 1))
                if h == 2:
                    use, _ = TURN.use(s, "elu0")
                    dve.wait_ge(turn_full, use + 1)
                nc.vector.scalar_tensor_tensor(out=elu[h % 2][:], in0=ez[h % 2][:], scalar=1.0, in1=z1[h % 2][:],
                                               op0=ALU.min, op1=ALU.max).then_inc(elu_made, 1)

            def layer_out(s, c):
                use, k = SUMS.use(s, "sum2", c)
                dve.wait_ge(sums_full, use + 1)
                settle(nc.vector.reciprocal(rz2[:, c:c + 1], sums_b[k][:, DIM:DIM + 1]))
                if c == 0:
                    dve.wait_ge(xb_made, s.back.n + 1)
                x1 = xb[s.back.slot][:, c, :]
                nc.vector.scalar_tensor_tensor(out=x1, in0=sums_b[k][:, 0:DIM], scalar=rz2[:, c:c + 1],
                                               in1=x1, op0=ALU.mult, op1=ALU.add).then_inc(sums_free, 1)

            def weights3(s, c):
                n = s.tail.n * NC + (c + 1)
                dve.wait_ge(e3_made, n)
                nc.vector.scalar_tensor_tensor(out=prob3[:, c, :], in0=maskT[s.tail.slot][:, c, :],
                                               scalar=empty[:, c:c + 1], in1=prob3[:, c, :], op0=ALU.max,
                                               op1=ALU.mult, accum_out=z3[:, c:c + 1]).then_inc(prob_full[2], 1)
                dve.wait_ge(prob_full[2], n)
                nc.vector.reciprocal(rz3[:, c:c + 1], z3[:, c:c + 1]).then_inc(rz3_made, 1)

            def leaky_sums(s, a):
                use, k = SUMS.use(s, "sum3", a)
                dve.wait_ge(small_made, s.tail.n * 2 + (a + 1))
                nc.vector.tensor_tensor(small[:, 2 * a:2 * a + 2, :], small[:, 2 * a:2 * a + 2, :],
                                        sums_b[k][:].rearrange("p (c f) -> p c f", c=2), ALU.max
                                        ).then_inc(sums_free, 1)

            def columns(name, s, src, sc):
                which = int(name) - 1
                use, _ = PROJ.use(s, "proj" + name, NC - 1)
                dve.wait_ge(proj_free, use + 1)
                nc.vector.tensor_copy(sc.cols[:, :, 0:1], src[:, :, DIM:DIM + 1])
                nc.vector.tensor_copy(sc.cols[:, :, 32:33], src[:, :, DIM + 1:DIM + 2]).then_inc(cols_made[which], 1)

            def step(s):
                begun = settled[0] = count_before(s, SETTLED)
                if not s.looped and s.t == 0:
                    prepare_w2_w3()
                if s.tail:
                    split(s, s.tail, 2, sc3)
                    use, k = ROWS.use(s, "shift3")
                    dve.wait_ge(rows_full, use + 1)
                    nc.vector.tensor_scalar(low_col[:], sc3.cols[:, :, 32], rows_b[k][:, 0:1], 0.0,
                                            ALU.subtract, ALU.max).then_inc(rows_free, 1)
                    dve.wait_ge(rows_free, use + 1)
                    nc.vector.tensor_scalar(keep[:], count[s.tail.slot][:], 1.0, None, ALU.min)
                    settle(nc.vector.tensor_scalar(low_col[:], low_col[:], -FALL, None, ALU.mult))
                    settle(nc.vector.tensor_scalar(empty[:], keep[:], -1.0, 1.0, ALU.mult, ALU.add))
                    use, k = ROWS.use(s, "q3")
                    dve.wait_ge(low_row_made, s.tail.n + 1)
                    for c in range(NC):
                        nc.vector.scalar_tensor_tensor(out=prob3[:, c, :], in0=low_row[:], scalar=low_col[:, c:c + 1],
                                                       in1=rows_b[k][:], op0=ALU.add, op1=ALU.max
                                                       ).then_inc(expo_made, 1)
                    nc.vector.engine_nop().then_inc(rows_free, 1)
                    weights3(s, 0)
                if s.front:
                    rows_of(s, s.front, "1", 0, sc1)
                if s.tail:
                    weights3(s, 1)
                    weights3(s, 2)
                if s.front:
                    split(s, s.front, 0, sc1)
                    shifted(s, "1", sc1)
                    use, _ = TURN.use(s, "mask", 1)
                    dve.wait_ge(turn_full, use + 1)
                    for c in range(NC):
                        own = mask[s.front.slot][:, c, c * P:(c + 1) * P]
                        last = nc.vector.tensor_tensor(own, own, ident_b[:], ALU.max)
                    settle(last)
                if s.tail:
                    weights3(s, 3)
                if s.after:
                    k = s.after.slot
                    dve.wait_ge(x_loaded[k], s.after.half * 16 + 16)
                    half_moments(norm1, x_in[k])
                if s.back:
                    columns("2", s, xl2, sc2)
                if s.front:
                    head_weights(s, 0, range(0, 2))
                if s.after:
                    moments(0, norm1)
                if s.front:
                    head_weights(s, 0, range(2, 4))
                if s.back:
                    rows_of(s, s.back, "2", 1, sc2)
                if s.tail:
                    leaky_sums(s, 0)
                if s.back:
                    split(s, s.back, 1, sc2)
                    shifted(s, "2", sc2)
                if s.tail:
                    leaky_sums(s, 1)
                if s.back:
                    weights(s, s.back, "q2", 0, 1, sc2, prob2, range(0, 2))
                if s.front:
                    head_out(0, 0, SUMS.use(s, "head0", 0))
                if s.back:
                    weights(s, s.back, "q2", 0, 1, sc2, prob2, range(2, 4))
                if s.front:
                    head_out(0, 1, SUMS.use(s, "head0", 1))
                    head_weights(s, 1, range(0, 2))
                if s.back:
                    layer_out(s, 0)
                if s.front:
                    head_weights(s, 1, range(2, 4))
                if s.back:
                    layer_out(s, 1)
                    if not s.front:
                        half_moments_x1(s, 0)
                if s.front:
                    elu_out(s, s.front, 0)
                    head_weights(s, 2, range(0, 2))
                if s.back:
                    layer_out(s, 2)
                    if not s.front:
                        half_moments_x1(s, 1)
                if s.front:
                    head_weights(s, 2, range(2, 4))
                if s.back:
                    layer_out(s, 3)
                    for c in range(NC) if s.front else range(NC - 2, NC):
                        half_moments_x1(s, c)
                if s.front:
                    head_out(1, 0, SUMS.use(s, "head1", 0))
                if s.back:
                    moments(1, norm2)
                if s.front:
                    head_out(1, 1, SUMS.use(s, "head1", 1))
                    head_weights(s, 3, range(0, 2))
                if s.back:
                    dve.wait_ge(rstd_made[1], s.back.n + 1)
                    for c in range(NC // 2):
                        last = nc.vector.tensor_scalar(norm2.out[:, c, :], xb[s.back.slot][:, c, :],
                                                       norm2.stats[:, c, 0:1], norm2.rstd[:, c:c + 1],
                                                       ALU.subtract, ALU.mult)
                    last.then_inc(hn_made[1], 1)
                if s.front:
                    elu_out(s, s.front, 1)
                    head_out(2, 0, SUMS.use(s, "head2", 0))
                    head_weights(s, 3, range(2, 4))
                    head_out(2, 1, SUMS.use(s, "head2", 1))
                    elu_out(s, s.front, 2)
                    head_out(3, 0, SUMS.use(s, "head3", 0))
                if not s.looped and s.t == -1:
                    prepare_w1()
                if s.front:
                    head_out(3, 1, SUMS.use(s, "head3", 1))
                if s.after:
                    k = s.after.slot
                    dve.wait_ge(adj_loaded, s.after.n * 16 + 16)
                    nc.vector.tensor_scalar(mask[k][:], adj_in[:], 0, None, ALU.is_gt).then_inc(mask_made, 1)
                if s.front:
                    elu_out(s, s.front, 3)
                if s.back:
                    columns("3", s, xl3, sc3)
                    rows_of(s, s.back, "3", 2, sc3)
                assert s.looped or settled[0] - begun == sum(SETTLED[g] for g in SETTLED if s.has(g))

            steps(dve, step)

        @block.tensor
        def _(pe):
            def turn_bank(s, name, i=0):
                use, b = TURN.use(s, name, i)
                if older(use):
                    pe.wait_ge(turn_free, use - 1)
                return turn_b[b]

            def rows_bank(s, name):
                use, b = ROWS.use(s, name)
                if older(use):
                    pe.wait_ge(rows_free, use - 1)
                return rows_b[b]

            def turn_nodes(s, b, name, which, norm):
                pe.wait_ge(hn_made[which], (b.n + 1) * (1 + which))
                for k in range(KC):
                    T = turn_bank(s, name, k)
                    for c in range(NC):
                        last = nc.tensor.transpose(T[:, c * P:(c + 1) * P], norm.out[:, c, k * P:(k + 1) * P], ident[:])
                    last.then_inc(turn_full, 1)

            def project(s, name, i, parts, c, w, wait=None):
                use, b = PROJ.use(s, name, i)
                if older(use):
                    pe.wait_ge(proj_free, use - 1)
                n, depth = w[0][0].shape[-1], len(w[0])
                for k in range(depth):
                    if k == depth - 1 and wait:
                        wait()
                    for a, v in ((0, 0), (0, 1), (1, 0)):
                        last = nc.tensor.matmul(proj_b[b][:, 0:n], parts[a][:, k, c * P:(c + 1) * P], w[v][k],
                                                start=(k == 0 and a == 0 and v == 0), stop=(k == depth - 1 and a == 1))
                last.then_inc(proj_full, 1)

            def rows(s, b, name, which, sc):
                if which == 0:
                    use, _ = PROJ.use(s, "proj1", 2 * NC - 1)
                    pe.wait_ge(proj_free, use + 1)
                else:
                    pe.wait_ge(cols_made[which], b.n + 1)
                R = rows_bank(s, "rows" + name)
                for c in range(NC):
                    last = nc.tensor.transpose(R[:, c * P:(c + 1) * P], sc.turned(c), ident[:])
                last.then_inc(rows_full, 1)

            def shift(s, b, name, which, sc):
                pe.wait_ge(diag_made[which], b.n + 1)
                R = rows_bank(s, "shift" + name)
                nc.tensor.matmul(R[:, 0:sc.heads], ones[:], sc.diag[:, 0:sc.heads], start=True, stop=True
                                 ).then_inc(rows_full, 1)

            def spread_row(s, b, name, i, which, sc):
                pe.wait_ge(split_made[which], b.n + 1)
                R = rows_bank(s, name)
                nc.tensor.matmul(R[:], pick[:, i, :], sc.split[:], start=True, stop=True).then_inc(rows_full, 1)

            def weigh(s, name, i, j, per_bank, which, weight, of, n, y, d, scaled=None):
                use, k = SUMS.use(s, name, i)
                if j == 0 and older(use):
                    pe.wait_ge(sums_free, use - 1)
                for c in range(NC):
                    if d == 0:
                        pe.wait_ge(prob_full[which], of + (c + 1))
                        if scaled:
                            pe.wait_ge(scaled, of + (c + 1))
                    last = nc.tensor.matmul(sums_b[k][:, j * n:(j + 1) * n], weight[:, c, d * P:(d + 1) * P], y(c),
                                            start=(c == 0), stop=(c == NC - 1))
                if j == per_bank - 1:
                    last.then_inc(sums_full, 1)

            def head(s, h, a, between=None):
                if a == 0:
                    pe.wait_ge(y1_made, s.front.n * HEADS + (h + 1))
                for j in range(2):
                    if j == 1 and between:
                        between()
                    weigh(s, f"head{h}", a, j, 2, 0, prob1[h % 2], s.front.n * (HEADS * NC) + h * NC, HEAD_DIM + 1,
                          lambda c: y1[:, c, h, :], 2 * a + j)

            def turn_elu(s, b, h):
                pe.wait_ge(elu_made, b.n * HEADS + (h + 1))
                T = turn_bank(s, f"elu{h}")
                for c in range(NC):
                    last = nc.tensor.transpose(T[:, c * P:(c + 1) * P], elu[h % 2][:, c, :], ident[:])
                last.then_inc(turn_full, 1)

            def proj1(s, c):
                for g in range(2):
                    project(s, "proj1", 2 * c + g, norm1.T, c, [[w[:, k, GROUP1[g]] for k in range(KC)] for w in w1])

            def proj2(s, c):
                project(s, "proj2", c, h2T, c, [[w[:, k, :] for k in range(HEADS)] for w in w2])

            def sum2(s, d):
                weigh(s, "sum2", d, 0, 1, 1, prob2, s.back.n * NC, DIM + 1, lambda c: xl2[:, c, 0:DIM + 1], d, y2_made)

            def sum3(s, d):
                weigh(s, "sum3", d // 2, d % 2, 2, 2, prob3, s.tail.n * NC, DIM, lambda c: xl3[:, c, 0:DIM], d, y3_made)

            def step(s):
                if s.front:
                    pe.wait_ge(lo_made, WHOLE.before(s)[0] - (HEADS + KC if s.looped or s.t > 1 else HEADS * s.t))
                    if not s.looped and s.t == 0:
                        pe.wait_ge(w1_ready, 1)
                        pe.wait_ge(features_split, 1)
                if s.front:
                    proj1(s, 0)
                    proj1(s, 1)
                if s.tail:
                    shift(s, s.tail, "3", 2, sc3)
                    spread_row(s, s.tail, "q3", 0, 2, sc3)
                if s.front:
                    proj1(s, 2)
                    proj1(s, 3)
                    pe.wait_ge(mask_made, s.front.n + 1)
                    for j in range(2):
                        T = turn_bank(s, "mask", j)[:].bitcast(BF16)
                        for k in range(2):
                            for c in range(NC):
                                at = k * NODES + c * P
                                last = nc.tensor.transpose(T[:, at:at + P],
                                                           mask[s.front.slot][:, c, (2 * j + k) * P:(2 * j + k + 1) * P],
                                                           ident_b[:])
                        last.then_inc(turn_full, 1)
                    rows(s, s.front, "1", 0, sc1)
                if s.back:
                    if not s.looped and s.t == 1:
                        pe.wait_ge(w_ready, 1)
                        pe.wait_ge(features_split, 3)
                    pe.wait_ge(lo_made, WHOLE.before(s)[0])
                    proj2(s, 0)
                    proj2(s, 1)
                if s.front:
                    shift(s, s.front, "1", 0, sc1)
                if s.back:
                    proj2(s, 2)
                if s.front:
                    spread_row(s, s.front, "q1_0", 0, 0, sc1)
                if s.back:
                    proj2(s, 3)
                if s.tail:
                    sum3(s, 0)
                if s.back:
                    rows(s, s.back, "2", 1, sc2)
                if s.tail:
                    sum3(s, 1)
                    sum3(s, 2)
                if s.back:
                    shift(s, s.back, "2", 1, sc2)
                if s.tail:
                    sum3(s, 3)
                def spread_q2():
                    if s.back:
                        spread_row(s, s.back, "q2", 0, 1, sc2)

                if s.front:
                    head(s, 0, 0, between=spread_q2)
                else:
                    spread_q2()
                if s.front:
                    spread_row(s, s.front, "q1_1", 1, 0, sc1)
                    head(s, 0, 1)
                if s.back:
                    sum2(s, 0)
                if s.front:
                    spread_row(s, s.front, "q1_2", 2, 0, sc1)
                if s.back:
                    for d in range(1, NC):
                        sum2(s, d)
                if s.after:
                    turn_nodes(s, s.after, "hn1", 0, norm1)
                if s.front:
                    head(s, 1, 0)
                    head(s, 1, 1)
                    spread_row(s, s.front, "q1_3", 3, 0, sc1)
                    turn_elu(s, s.front, 0)
                    head(s, 2, 0)
                    head(s, 2, 1)
                if s.back:
                    turn_nodes(s, s.back, "hn2", 1, norm2)
                if s.front:
                    head(s, 3, 0)
                    turn_elu(s, s.front, 1)
                    head(s, 3, 1)
                    turn_elu(s, s.front, 2)
                if s.back:
                    use, _ = WHOLE.use(s, "hn2", KC - 1)
                    pe.wait_ge(lo_made, use + 1)
                    for c in range(NC):
                        project(s, "proj3", c, norm2.T, c, [[w[:, k, :] for k in range(KC)] for w in w3])
                if s.front:
                    turn_elu(s, s.front, 3)
                if s.back:
                    rows(s, s.back, "3", 2, sc3)

            pe.wait_ge(pool_consts, 2)
            steps(pe, step)


_INS = ["x", "adj", "L0_gnn_W1", "L0_gnn_att_src1", "L0_gnn_att_dst1", "L0_gnn_b1", "L0_gnn_W2",
        "L0_gnn_att_src2", "L0_gnn_att_dst2", "L0_gnn_b2", "L1_gnn_W", "L1_gnn_a"]


def kernel(**inputs):
    import numpy as _np
    import concourse.bacc as _bacc
    from concourse import mybir as _mybir
    from concourse.bass_utils import run_bass_kernel_spmd as _run

    nc = _bacc.Bacc("TRN2", target_bir_lowering=False, num_devices=1)
    arrays, args = {}, []
    for name in _INS:
        a = _np.ascontiguousarray(inputs[name])
        arrays[f"in_{name}"] = a
        args.append(nc.dram_tensor(f"in_{name}", a.shape, _mybir.dt.from_np(a.dtype), kind="ExternalInput").ap())
    out = nc.dram_tensor("out_x", (BATCHES, NODES, DIM), F32, kind="ExternalOutput").ap()
    gat_block(nc, *args, out)
    r = _run(nc, [arrays], core_ids=[0])
    return r.results[0]["out_x"]
```
